# Optimizing a Trainium2 kernel written in Bass

```python
import numpy as np
import jax
import jax.numpy as jnp

def _softmax(x, axis=-1):
    return jax.nn.softmax(x, axis=axis)

def _gelu(x):
    return jax.nn.gelu(x, approximate=True)

def _silu(x):
    return jax.nn.silu(x)

def _sigmoid(x):
    return jax.nn.sigmoid(x)

def _layernorm(x, axis=-1, eps=1e-05):
    m = jnp.mean(x, axis=axis, keepdims=True)
    v = jnp.var(x, axis=axis, keepdims=True)
    return (x - m) / jnp.sqrt(v + eps)

def _scatter_add(tgt, idx, src, axis=0):
    return tgt.at[idx].add(src)

def _segment_sum(src, seg, n):
    return jax.ops.segment_sum(src, seg, n)
kernel_name = 'mk_vit_tower_d1_tok_img768_r4_87a2d4'

def setup_inputs(seed: int=0):
    np.random.seed(seed)
    _w = jnp.asarray

    def _rec_inputs():
        import jax
        import jax.numpy as jnp
        _rk = jax.random.key(seed)
        x = jax.random.uniform(jax.random.fold_in(_rk, 1), (16, 3, 96, 96), jnp.float32, 0.0, 1)
        return x
    x = _rec_inputs()

    def _L0_tok_setup():
        import jax, jax.numpy as jnp
        import numpy as np
        B, C, H, W, P, D = (32, 3, 96, 96, 16, 192)
        N = H // P * (W // P)
        key = jax.random.key(seed)
        k0, k1, k2, k3 = jax.random.split(key, 4)
        x = jax.random.uniform(k0, (B, C, H, W), dtype=jnp.float32)
        proj_w = jax.random.normal(k1, (D, P * P * C), dtype=jnp.float32) * 0.02
        proj_b = jnp.zeros((D,), jnp.float32)
        cls_token = jax.random.normal(k2, (1, 1, D), dtype=jnp.float32)
        pos_embedding = jax.random.normal(k3, (1, N + 1, D), dtype=jnp.float32)
        return {'x': x, 'proj_w': proj_w, 'proj_b': proj_b, 'cls_token': cls_token, 'pos_embedding': pos_embedding}
    _L0_tok_all = _L0_tok_setup()
    _L0_tok_in = {k: v for k, v in _L0_tok_all.items() if k in ('proj_w', 'proj_b', 'cls_token', 'pos_embedding')}
    del _L0_tok_all

    def _L0_attn_setup():
        import jax, jax.numpy as jnp
        import numpy as np
        import math
        B, N, C = (8, 1024, 192)
        H = 12
        DH = C // H
        M = 64
        LN_EPS = 1e-05

        def _phi(t, random_features):
            norm_sq = 0.5 * jnp.sum(t * t, axis=-1, keepdims=True)
            proj = jnp.einsum('bhnd,md->bhnm', t, random_features)
            return jnp.exp(proj - norm_sq) * (1.0 / math.sqrt(M))
        key = jax.random.key(seed)
        ks = jax.random.split(key, 7)
        x = jax.random.normal(ks[0], (B, N, C), dtype=jnp.float32)
        W_qkv = jax.random.normal(ks[1], (C, 3 * C), dtype=jnp.float32) * (1.0 / math.sqrt(C))
        W_proj = jax.random.normal(ks[2], (C, C), dtype=jnp.float32) * (1.0 / math.sqrt(C))
        b_proj = jnp.zeros((C,), dtype=jnp.float32)
        gamma = jnp.ones((C,), dtype=jnp.float32)
        beta = jnp.zeros((C,), dtype=jnp.float32)
        random_features = jax.random.normal(ks[3], (M, DH), dtype=jnp.float32) / math.sqrt(DH)
        return {'x': x, 'W_qkv': W_qkv, 'W_proj': W_proj, 'b_proj': b_proj, 'gamma': gamma, 'beta': beta, 'random_features': random_features}
    _L0_attn_all = _L0_attn_setup()
    _L0_attn_in = {k: v for k, v in _L0_attn_all.items() if k in ('W_qkv', 'W_proj', 'b_proj', 'gamma', 'beta', 'random_features')}
    del _L0_attn_all

    def _L0_ffn_setup():
        import jax, jax.numpy as jnp
        import numpy as np
        NUM_EXPERTS = 8
        TOP_K = 2
        CAP_FACTOR = 1.0
        D_MODEL = 192
        D_FF = 768
        key = jax.random.key(seed)
        k0, k1, k2, k3 = jax.random.split(key, 4)
        B, S, D = (1, 512, D_MODEL)
        inputs = jax.random.normal(k0, (B, S, D), dtype=jnp.float32)
        router_w = jax.random.normal(k1, (NUM_EXPERTS, D), dtype=jnp.float32) * D ** (-0.5)
        w1 = jax.random.normal(k2, (NUM_EXPERTS, D, D_FF), dtype=jnp.float32) * D ** (-0.5)
        w2 = jax.random.normal(k3, (NUM_EXPERTS, D_FF, D), dtype=jnp.float32) * D_FF ** (-0.5)
        return {'inputs': inputs, 'router_w': router_w, 'w1': w1, 'w2': w2}
    _L0_ffn_all = _L0_ffn_setup()
    _L0_ffn_in = {k: v for k, v in _L0_ffn_all.items() if k in ('router_w', 'w1', 'w2')}
    del _L0_ffn_all
    return {'x': x, 'L0_tok_proj_w': _L0_tok_in['proj_w'], 'L0_tok_proj_b': _L0_tok_in['proj_b'], 'L0_tok_cls_token': _L0_tok_in['cls_token'], 'L0_tok_pos_embedding': _L0_tok_in['pos_embedding'], 'L0_attn_W_qkv': _L0_attn_in['W_qkv'], 'L0_attn_W_proj': _L0_attn_in['W_proj'], 'L0_attn_b_proj': _L0_attn_in['b_proj'], 'L0_attn_gamma': _L0_attn_in['gamma'], 'L0_attn_beta': _L0_attn_in['beta'], 'L0_attn_random_features': _L0_attn_in['random_features'], 'L0_ffn_router_w': _L0_ffn_in['router_w'], 'L0_ffn_w1': _L0_ffn_in['w1'], 'L0_ffn_w2': _L0_ffn_in['w2']}

def reference(x, L0_tok_proj_w, L0_tok_proj_b, L0_tok_cls_token, L0_tok_pos_embedding, L0_attn_W_qkv, L0_attn_W_proj, L0_attn_b_proj, L0_attn_gamma, L0_attn_beta, L0_attn_random_features, L0_ffn_router_w, L0_ffn_w1, L0_ffn_w2):
    import jax
    import jax.numpy as jnp

    def _L0_tok_ref(x, proj_w, proj_b, cls_token, pos_embedding):
        import jax, jax.numpy as jnp
        import numpy as np
        B, C, H, W, P, D = (32, 3, 96, 96, 16, 192)
        N = H // P * (W // P)
        b, c, h, w = x.shape
        hp, wp = (h // P, w // P)
        patches = x.reshape(b, c, hp, P, wp, P).transpose(0, 2, 4, 1, 3, 5).reshape(b, hp * wp, c * P * P)
        tok = jnp.einsum('bnk,dk->bnd', patches, proj_w) + proj_b
        cls = jnp.broadcast_to(cls_token, (b, 1, cls_token.shape[-1]))
        z0 = jnp.concatenate([cls, tok], axis=1) + pos_embedding
        return z0

    def _L0_attn_ref(x, W_qkv, W_proj, b_proj, gamma, beta, random_features):
        import jax, jax.numpy as jnp
        import numpy as np
        import math
        B, N, C = (8, 1024, 192)
        H = 12
        DH = C // H
        M = 64
        LN_EPS = 1e-05

        def _phi(t, random_features):
            norm_sq = 0.5 * jnp.sum(t * t, axis=-1, keepdims=True)
            proj = jnp.einsum('bhnd,md->bhnm', t, random_features)
            return jnp.exp(proj - norm_sq) * (1.0 / math.sqrt(M))
        b, n, c = x.shape
        qkv = (x @ W_qkv).reshape(b, n, 3, H, DH)
        qkv = jnp.transpose(qkv, (2, 0, 3, 1, 4))
        q, k, v = (qkv[0], qkv[1], qkv[2])
        q_p = _phi(q, random_features)
        k_p = _phi(k, random_features)
        kv = jnp.einsum('bhnm,bhnd->bhmd', k_p, v)
        out = jnp.einsum('bhnm,bhmd->bhnd', q_p, kv)
        k_sum = jnp.sum(k_p, axis=2)
        normalizer = jnp.einsum('bhnm,bhm->bhn', q_p, k_sum)[..., None]
        out = out / (normalizer + 1e-06)
        x_attn = jnp.transpose(out, (0, 2, 1, 3)).reshape(b, n, c)
        x_attn = x_attn @ W_proj + b_proj
        y = x + x_attn
        mu = jnp.mean(y, axis=-1, keepdims=True)
        var = jnp.mean(jnp.square(y - mu), axis=-1, keepdims=True)
        return (y - mu) * jax.lax.rsqrt(var + LN_EPS) * gamma + beta

    def _L0_ffn_ref(inputs, router_w, w1, w2):
        import jax, jax.numpy as jnp
        import numpy as np
        NUM_EXPERTS = 8
        TOP_K = 2
        CAP_FACTOR = 1.0
        D_MODEL = 192
        D_FF = 768
        B, S, D = inputs.shape
        x = inputs.reshape(-1, D)
        N = x.shape[0]
        logits = x @ router_w.T
        probs = jax.nn.softmax(logits.astype(jnp.float32), axis=-1)
        weights, sel = jax.lax.top_k(probs, TOP_K)
        cap = int(CAP_FACTOR * N * TOP_K) + 1
        n_real = N * TOP_K
        expert_flat = sel.reshape(-1)
        weight_flat = weights.reshape(-1)
        token_idx = jnp.repeat(jnp.arange(N), TOP_K)
        pad = cap - n_real
        expert_flat = jnp.pad(expert_flat, (0, pad))
        weight_flat = jnp.pad(weight_flat, (0, pad))
        token_idx = jnp.pad(token_idx, (0, pad))
        valid = jnp.arange(cap) < n_real
        toks = x[token_idx]

        def mlp(w1e, w2e):
            return jax.nn.gelu(toks @ w1e) @ w2e
        ys = jax.vmap(mlp)(w1, w2)
        gate = (weight_flat * valid.astype(weight_flat.dtype)).astype(toks.dtype)
        res = ys[expert_flat, jnp.arange(cap)] * gate[:, None]
        out = jnp.zeros((N, D), dtype=inputs.dtype).at[token_idx].add(res)
        return out.reshape(B, S, D)
    h = _L0_tok_ref(x, L0_tok_proj_w, L0_tok_proj_b, L0_tok_cls_token, L0_tok_pos_embedding)
    h = h + _L0_attn_ref(_layernorm(h, axis=-1), L0_attn_W_qkv, L0_attn_W_proj, L0_attn_b_proj, L0_attn_gamma, L0_attn_beta, L0_attn_random_features)
    h = h + _L0_ffn_ref(_layernorm(h, axis=-1), L0_ffn_router_w, L0_ffn_w1, L0_ffn_w2)
    return h

_drawn_inputs = setup_inputs


def setup_inputs(seed=0):
    import zlib

    import numpy as np

    out = dict(_drawn_inputs(seed))
    spreads = {'L0_tok_proj_b': (0.0, 0.1),
     'L0_attn_b_proj': (0.0, 0.1),
     'L0_attn_gamma': (1.0, 0.2),
     'L0_attn_beta': (0.0, 0.1)}
    factors = {}
    for name, (base, spread) in spreads.items():
        noise = np.random.default_rng([zlib.crc32(name.encode()), seed]).standard_normal(out[name].shape)
        drawn = base * np.exp(spread * noise) if base else spread * noise
        out[name] = jnp.asarray(drawn.astype(out[name].dtype))
    for name, factor in factors.items():
        out[name] = (out[name] * factor).astype(out[name].dtype)
    return out
```

```python
from contextlib import ExitStack

import numpy as np

import concourse.bass as bass
from concourse import mybir
from concourse.alu_op_type import AluOpType as ALU

ACT = mybir.ActivationFunctionType
AX = mybir.AxisListType
F32 = mybir.dt.float32

B, C, IMG, PATCH = 16, 3, 96, 16
NP = (IMG // PATCH) ** 2
N = NP + 1
TOK = B * N
HALF = TOK // 2
D = 192
DR = D - 128
KC = PATCH * PATCH * C // 128
T = -(-TOK // 128)
TP = 128 * T
LAST = TOK - 128 * (T - 1)
H, DH, M = 12, 16, 64
PAIRS = H // 2
HG = 4
NG = H // HG
IT = 3
S = -(-B // IT)
VW = DH + 1
E, F = 8, 768
FC = F // 128
LN_EPS = 1e-5
DEN_EPS = 1e-6

A_QK, A_V, A_RF, A_MASK = 0, NG * 128, NG * 128 + D, NG * 128 + D + HG * M
A_END = A_MASK + 4
B_P, B_R, B_GAM, B_BET, B_TRI = 0, D, D + E, 2 * D + E, 3 * D + E
B_END = B_TRI + E * E
R_QK, R_V, R_P, R_R = 0, NG * 128, NG * 128 + D, NG * 128 + 2 * D
R_END = R_R + E


def vit_tower(nc, xT, embed_w, pos_w, ident_w, att_a, att_b, att_r, w1a, w1b, w2, out):
    ctx = ExitStack()
    with ctx:
        def sb(name, shape):
            return ctx.enter_context(nc.sbuf_tensor(name, shape, F32))

        def psum(name, shape):
            return ctx.enter_context(nc.psum_tensor(name, shape, F32))

        def sem(name):
            return ctx.enter_context(nc.semaphore(name))

        tokP = psum("tokP", [128, 2, 512])
        turnP = psum("turnP", [128, 2, 512])
        featP = psum("featP", [128, 2, 2, 512])

        x_sb = sb("x_sb", [128, T, KC * 128])
        embed_sb = sb("embed_sb", [128, KC, D])
        pos_sb = sb("pos_sb", [N + 2, D + TP])
        ident = sb("ident", [128, 128])
        wa = sb("wa", [128, A_END])
        wb = sb("wb", [128, B_END])
        wr = sb("wr", [DR + 1, R_END])

        h = sb("h", [128, T, D])
        hb = sb("hb", [128, T, D])
        xn1 = sb("xn1", [128, T, D])
        xTa = sb("xTa", [128, TP])
        xTb = sb("xTb", [DR, TP])
        stat = sb("stat", [128, 3, T, 6])
        mv = sb("mv", [128, 3, T, 2])
        ve = sb("ve", [128, 3, T])
        rstd = sb("rstd", [128, 3, T])
        mhalf = sb("mhalf", [128, 1])
        qa = sb("qa", [128, NG, TOK])
        ka = sb("ka", [128, NG, TOK])
        qp = sb("qp", [128, PAIRS, TP])
        kp = sb("kp", [IT * N, 2, H * M])
        vm = sb("vm", [IT * N, 2, IT, H, VW])
        kv = sb("kv", [128, B, PAIRS, 2 * VW])
        den = sb("den", [128, 4, 2 * H])
        rden = sb("rden", [128, 4, 2 * H])
        o = sb("o", [128, 4, 2 * H, DH])
        oTa = sb("oTa", [128, TP])
        oTb = sb("oTb", [DR + 1, TP])
        y = sb("y", [128, T, D])
        yg = sb("yg", [128, T, D])
        res = sb("res", [128, T, D])
        xn2 = sb("xn2", [128, T, D])
        lmax = sb("lmax", [128, T])
        lg = sb("lg", [128, T, E])
        pe_ = sb("pexp", [128, T, E])
        psumr = sb("psumr", [128, T])
        prec = sb("prec", [128, T])
        prob = sb("prob", [128, T, E])
        beats = sb("beats", [128, T, E, E])
        ties = sb("ties", [128, T, E, E])
        rank = sb("rank", [128, T, E])
        gate = sb("gate", [128, T, E])
        w1a_sb = sb("w1a_sb", [128, 2, F])
        w1b_sb = sb("w1b_sb", [DR, 2, F])
        w2_sb = sb("w2_sb", [128, 2, FC, D])
        hid = sb("hid", [128, 2, FC, TP])

        x_landed = [sem(f"x_landed{t}") for t in range(T)]
        embed_landed = sem("embed_landed")
        pos_landed = sem("pos_landed")
        ident_landed = sem("ident_landed")
        wa_landed = sem("wa_landed")
        wb_landed = sem("wb_landed")
        wr_landed = sem("wr_landed")
        w1_landed = [sem(f"w1_landed{u}") for u in range(2)]
        w2_landed = [sem(f"w2_landed{u}") for u in range(2)]
        out_stored = sem("out_stored")
        pool_const = sem("pool_const")
        embed_done = sem("embed_done")
        h_ready = sem("h_ready")
        ve_ready = [sem(f"ve_ready{n}") for n in range(3)]
        rstd_ready = [sem(f"rstd_ready{n}") for n in range(3)]
        hb_ready = sem("hb_ready")
        xn_ready = sem("xn_ready")
        turned = sem("turned")
        xT_ready = sem("xT_ready")
        qk_done = sem("qk_done")
        q_copied = sem("q_copied")
        k_copied = sem("k_copied")
        q_ready = sem("q_ready")
        k_ready = sem("k_ready")
        v_done = sem("v_done")
        vm_ready = sem("vm_ready")
        kproj_done = sem("kproj_done")
        qproj_done = sem("qproj_done")
        kp_ready = sem("kp_ready")
        qp_ready = sem("qp_ready")
        kv_done = sem("kv_done")
        kv_low = sem("kv_low")
        kv_high = sem("kv_high")
        att_done = sem("att_done")
        o_ready = sem("o_ready")
        o_turned = sem("o_turned")
        oT_ready = sem("oT_ready")
        proj_done = sem("proj_done")
        y_ready = sem("y_ready")
        router_done = sem("router_done")
        lg_ready = sem("lg_ready")
        pexp_ready = sem("pexp_ready")
        up_done = sem("up_done")
        hid_ready = sem("hid_ready")
        down_done = sem("down_done")
        summed = sem("summed")
        dve_step = sem("dve_step")

        block = ctx.enter_context(nc.Block())

        @block.sync
        def _(sp):
            sp.dma_start(embed_sb[:].rearrange("p c d -> p (c d)"), embed_w).then_inc(embed_landed, 16)
            sp.dma_start(x_sb[:, 0, :], xT[0]).then_inc(x_landed[0], 16)
            sp.dma_start(pos_sb[:], pos_w).then_inc(pos_landed, 16)
            sp.dma_start(x_sb[:, 1, :], xT[1]).then_inc(x_landed[1], 16)
            sp.dma_start(ident[:], ident_w).then_inc(ident_landed, 16)
            for t in range(2, T):
                sp.dma_start(x_sb[:, t, :], xT[t]).then_inc(x_landed[t], 16)
            sp.dma_start(wa[:], att_a).then_inc(wa_landed, 16)
            sp.dma_start(wr[:], att_r).then_inc(wr_landed, 16)
            sp.dma_start(wb[:], att_b).then_inc(wb_landed, 16)
            for u in range(2):
                sp.dma_start(w1a_sb[:, u, :], w1a[u]).then_inc(w1_landed[u], 16)
                sp.dma_start(w1b_sb[:, u, :], w1b[u]).then_inc(w1_landed[u], 16)
                sp.dma_start(w2_sb[:, u], w2[u]).then_inc(w2_landed[u], 16)
            with sp.Fori(1, E // 2) as i:
                for u in range(2):
                    sp.wait_ge(up_done, i * (2 * FC) + (u - 1) * FC)
                    sp.dma_start(w1a_sb[:, u, :], w1a[bass.ds(i * 2 + u, 1)].rearrange("e p f -> (e p) f")).then_inc(w1_landed[u], 16)
                    sp.dma_start(w1b_sb[:, u, :], w1b[bass.ds(i * 2 + u, 1)].rearrange("e p f -> (e p) f")).then_inc(w1_landed[u], 16)
                    sp.wait_ge(down_done, i * (2 * T) + (u - 1) * T)
                    sp.dma_start(w2_sb[:, u].rearrange("p c d -> p (c d)"), w2[bass.ds(i * 2 + u, 1)].rearrange("e p c d -> (e p) (c d)")).then_inc(w2_landed[u], 16)
            for t in range(T):
                n = 128 if t < T - 1 else LAST
                sp.wait_ge(summed, (E - 1) * T + t + 1)
                sp.dma_start(out[128 * t:128 * t + n, :], res[0:n, t, :]).then_inc(out_stored, 16)
            sp.wait_ge(out_stored, 16 * T)

        @block.gpsimd
        def _(pool):
            nc.gpsimd.memset(mhalf[:], -0.5).then_inc(pool_const, 1)
            nc.gpsimd.memset(kv[:], 0.0).then_inc(pool_const, 1)
            nc.gpsimd.memset(qp[:, :, TOK:TP], 0.0).then_inc(pool_const, 1)
            nc.gpsimd.memset(oTa[:, TOK:TP], 0.0).then_inc(pool_const, 1)
            nc.gpsimd.memset(oTb[0:DR, TOK:TP], 0.0).then_inc(pool_const, 1)
            nc.gpsimd.memset(hid[:, :, :, TOK:TP], 0.0).then_inc(pool_const, 1)
            pool.wait_ge(pool_const, 6)
            nc.gpsimd.memset(oTb[DR:DR + 1, :], 1.0).then_inc(pool_const, 1)
            pool.wait_ge(pool_const, 7)

            def inverse_root(norm, t):
                pool.wait_ge(ve_ready[norm], t + 1)
                nc.gpsimd.tensor_tensor(rstd[:, norm, t:t + 1], ve[:, norm, t:t + 1], mhalf[:], ALU.pow).then_inc(rstd_ready[norm], 1)

            for t in range(T):
                inverse_root(0, t)
            pool.wait_ge(wb_landed, 16)
            for t in range(T):
                nc.gpsimd.tensor_tensor(hb[:, t, :], h[:, t, :], wb[:, B_BET:B_BET + D], ALU.add).then_inc(hb_ready, 1)
            for t in range(T + 1):
                if t < T:
                    inverse_root(1, t)
                if t >= 1:
                    inverse_root(2, t - 1)

        @block.scalar
        def _(act):
            for t in range(T + 1):
                if t < T:
                    act.wait_ge(embed_done, t + 1)
                    nc.scalar.copy(h[:, t, :], tokP[:, t % 2, 0:D]).then_inc(h_ready, 1)
                if t >= 1:
                    act.wait_ge(turned, t)
                    c = slice(128 * (t - 1), 128 * t)
                    nc.scalar.copy(xTa[:, c], turnP[:, (t - 1) % 2, 0:128]).then_inc(xT_ready, 1)
                    nc.scalar.copy(xTb[:, c], turnP[0:DR, (t - 1) % 2, 128:256]).then_inc(xT_ready, 1)
            for g in range(NG):
                act.wait_ge(qk_done, g + 1)
                nc.scalar.copy(ka[0:64, g, :].rearrange("p (n t) -> p n t", n=2), featP[64:128, g % 2, :, 0:HALF]).then_inc(k_copied, 1)
                act.wait_ge(k_copied, g + 1)
                nc.scalar.activation(ka[64:128, g, :], ka[0:64, g, :], ACT.Square).then_inc(k_ready, 1)

            def kv_rows_high(s):
                n = min(IT, B - IT * s)
                act.wait_ge(kv_done, s + 1)
                nc.scalar.activation(
                    kv[64:128, IT * s:IT * s + n, :, VW:2 * VW].rearrange("p i h v -> p h i v"),
                    turnP[64:128].rearrange("p b (h c) -> p (b h) c", c=128)[:, 0:PAIRS, 0:2 * VW * n].rearrange("p h (i v) -> p h i v", i=n)[:, :, :, VW:2 * VW],
                    ACT.Copy, scale=1.0 / M).then_inc(kv_high, 1)

            act.wait_ge(pool_const, 7)
            for s in range(S):
                rows = min(IT, B - IT * s) * N
                act.wait_ge(kproj_done, s + 1)
                if s >= 2:
                    act.wait_ge(kv_done, s - 1)
                nc.scalar.activation(kp[0:rows, s % 2, :], featP[0:rows, 0].rearrange("p b c -> p (b c)")[:, 0:H * M], ACT.Exp).then_inc(kp_ready, 1)
                act.wait_ge(qproj_done, s + 1)
                nc.scalar.activation(qp[:, s, 0:TOK].rearrange("p (n t) -> p n t", n=2), featP[:, 1, :, 0:HALF], ACT.Exp).then_inc(qp_ready, 1)
                if s >= 1:
                    kv_rows_high(s - 1)
            kv_rows_high(S - 1)
            for k in range(4):
                act.wait_ge(o_turned, k + 1)
                c = slice(4 * N * k, 4 * N * (k + 1))
                for dst, at, rows in ((oTa, 0, 128), (oTb, 256, DR)):
                    nc.scalar.copy(dst[0:rows, c].rearrange("p (i n) -> p i n", n=N),
                                   turnP[0:rows, k % 2, at:at + 256].rearrange("p (i n) -> p i n", n=64)[:, :, 0:N]).then_inc(oT_ready, 1)
            for t in range(T):
                act.wait_ge(turned, T + t + 1)
                c = slice(128 * t, 128 * (t + 1))
                nc.scalar.copy(xTa[:, c], turnP[:, t % 2, 0:128]).then_inc(xT_ready, 1)
                nc.scalar.copy(xTb[:, c], turnP[0:DR, t % 2, 128:256]).then_inc(xT_ready, 1)
            act.wait_ge(lg_ready, 1)
            nc.scalar.activation(pe_[:], lg[:], ACT.Exp).then_inc(pexp_ready, 1)

            def gelu(e, u, j):
                act.wait_ge(up_done, e * FC + j + 1)
                nc.scalar.activation(hid[:, u, j, 0:TOK].rearrange("p (n t) -> p n t", n=2), featP[:, j % 2, :, 0:HALF],
                                     ACT.Gelu_apprx_tanh).then_inc(hid_ready, 1)

            for u in range(2):
                for j in range(FC):
                    gelu(u, u, j)
            with act.Fori(1, E // 2) as i:
                for u in range(2):
                    act.wait_ge(down_done, i * (2 * T) + (u - 1) * T)
                    for j in range(FC):
                        gelu(i * 2 + u, u, j)

        @block.tensor
        def _(pe):
            def turn(src, t, n):
                pe.wait_ge(xn_ready, n + 1)
                if n >= 2:
                    pe.wait_ge(xT_ready, 2 * (n - 1))
                pe.transpose(turnP[:, t % 2, 0:128], src[:, t, 0:128], ident[:])
                pe.transpose(turnP[0:DR, t % 2, 128:256], src[:, t, 128:D], ident[:]).then_inc(turned, 1)

            pe.wait_ge(embed_landed, 16)
            for t in range(T):
                pe.wait_ge(x_landed[t], 16)
                if t >= 2:
                    pe.wait_ge(h_ready, t - 1)
                for c in range(KC):
                    pe.matmul(tokP[:, t % 2, 0:D], x_sb[:, t, 128 * c:128 * (c + 1)], embed_sb[:, c, :], start=(c == 0), stop=False)
                if t == 0:
                    pe.wait_ge(pos_landed, 16)
                pe.matmul(tokP[:, t % 2, 0:D], pos_sb[:, D + 128 * t:D + 128 * (t + 1)], pos_sb[:, 0:D], start=False, stop=True).then_inc(embed_done, 1)
                if t == 0:
                    pe.wait_ge(ident_landed, 16)
                else:
                    turn(xn1, t - 1, t - 1)
            turn(xn1, T - 1, T - 1)

            pe.wait_ge(wa_landed, 16)
            pe.wait_ge(wr_landed, 16)
            pe.wait_ge(xT_ready, 2 * T)
            for g in range(NG):
                if g >= 2:
                    pe.wait_ge(q_copied, g - 1)
                    pe.wait_ge(k_copied, g - 1)
                for n in range(2):
                    c = slice(HALF * n, HALF * (n + 1))
                    pe.matmul(featP[:, g % 2, n, 0:HALF], wa[:, A_QK + 128 * g:A_QK + 128 * (g + 1)], xTa[:, c], start=True, stop=False)
                    mm = pe.matmul(featP[:, g % 2, n, 0:HALF], wr[0:DR, R_QK + 128 * g:R_QK + 128 * (g + 1)], xTb[:, c], start=False, stop=True)
                mm.then_inc(qk_done, 1)

            def key_sums(s):
                n = min(IT, B - IT * s)
                pe.wait_ge(kp_ready, s + 1)
                pe.wait_ge(vm_ready, s + 1)
                if s >= 1:
                    pe.wait_ge(kv_low, s)
                    pe.wait_ge(kv_high, s)
                for p in range(PAIRS):
                    mm = pe.matmul(turnP[:, p // 4, 128 * (p % 4):128 * (p % 4) + 2 * VW * n].rearrange("p (i v) -> p i v", i=n),
                                   kp[0:n * N, s % 2, 128 * p:128 * (p + 1)],
                                   vm[0:n * N, s % 2, 0:n, 2 * p:2 * p + 2, :].rearrange("p i h v -> p i (h v)"), start=True, stop=True)
                mm.then_inc(kv_done, 1)

            for s in range(S):
                rows = min(IT, B - IT * s) * N
                c = slice(IT * N * s, IT * N * s + rows)
                if s >= 2:
                    pe.wait_ge(vm_ready, s - 1)
                pe.matmul(tokP[0:rows, s % 2, 0:D], xTa[:, c], wa[:, A_V:A_V + D], start=True, stop=False)
                pe.matmul(tokP[0:rows, s % 2, 0:D], xTb[:, c], wr[0:DR, R_V:R_V + D], start=False, stop=True).then_inc(v_done, 1)
                if s == 0:
                    pe.wait_ge(k_ready, NG)
                    pe.wait_ge(q_ready, NG)
                else:
                    pe.wait_ge(kp_ready, s)
                for g in range(NG):
                    mm = pe.matmul(featP[0:rows, 0, g // 2, 256 * (g % 2):256 * (g % 2) + HG * M], ka[:, g, c], wa[:, A_RF:A_RF + HG * M], start=True, stop=True)
                mm.then_inc(kproj_done, 1)
                if s >= 1:
                    pe.wait_ge(qp_ready, s)
                for n in range(2):
                    mm = pe.matmul(featP[:, 1, n, 0:HALF], wa[:, A_RF + 128 * (s % 2):A_RF + 128 * (s % 2 + 1)],
                                   qa[:, s // 2, HALF * n:HALF * (n + 1)], start=True, stop=True)
                mm.then_inc(qproj_done, 1)
                if s >= 1:
                    key_sums(s - 1)
            key_sums(S - 1)

            pe.wait_ge(qp_ready, S)
            pe.wait_ge(kv_low, S)
            pe.wait_ge(kv_high, S)
            def turn_o(k):
                pe.wait_ge(o_ready, k + 1)
                if k >= 2:
                    pe.wait_ge(oT_ready, 2 * (k - 1))
                for gg in range(2):
                    f = o[:, k, H * gg:H * (gg + 1), :].rearrange("p h d -> p (h d)")
                    pe.transpose(turnP[:, k % 2, 128 * gg:128 * (gg + 1)], f[:, 0:128], ident[:])
                    mm = pe.transpose(turnP[0:DR, k % 2, 256 + 128 * gg:256 + 128 * (gg + 1)], f[:, 128:D], ident[:])
                mm.then_inc(o_turned, 1)

            for k in range(4):
                for gg in range(2):
                    for half in range(2):
                        b = 4 * k + 2 * gg + half
                        for p in range(PAIRS):
                            at = 2 * VW * (PAIRS * gg + p)
                            mm = pe.matmul(featP[64 * half:64 * (half + 1), k // 2, k % 2, at:at + 2 * VW],
                                           qp[:, p, N * b:N * b + 64], kv[:, b, p, :], start=True, stop=True)
                mm.then_inc(att_done, 1)
                if k >= 1:
                    turn_o(k - 1)
            turn_o(3)

            pe.wait_ge(wb_landed, 16)
            for t in range(T):
                pe.wait_ge(oT_ready, 2 * (-(-min(128 * (t + 1), TOK) // (4 * N))))
                if t >= 2:
                    pe.wait_ge(y_ready, t - 1)
                c = slice(128 * t, 128 * (t + 1))
                pe.matmul(tokP[:, t % 2, 0:D], oTa[:, c], wb[:, B_P:B_P + D], start=True, stop=False)
                pe.matmul(tokP[:, t % 2, 0:D], oTb[:, c], wr[:, R_P:R_P + D], start=False, stop=True).then_inc(proj_done, 1)

            for t in range(T):
                turn(xn2, t, T + t)

            pe.wait_ge(xT_ready, 4 * T)
            for t in range(T):
                c = slice(128 * t, 128 * (t + 1))
                pe.matmul(tokP[:, 0, E * t:E * (t + 1)], xTa[:, c], wb[:, B_R:B_R + E], start=True, stop=False)
                mm = pe.matmul(tokP[:, 0, E * t:E * (t + 1)], xTb[:, c], wr[0:DR, R_R:R_R + E], start=False, stop=True)
            mm.then_inc(router_done, 1)

            def up(e, u, j, first=False):
                if j == 0:
                    pe.wait_ge(w1_landed[u], (e - u) * 16 + 32)
                if not (first and j < 2):
                    pe.wait_ge(hid_ready, e * FC + j - 1)
                for n in range(2):
                    c = slice(HALF * n, HALF * (n + 1))
                    pe.matmul(featP[:, j % 2, n, 0:HALF], w1a_sb[:, u, 128 * j:128 * (j + 1)], xTa[:, c], start=True, stop=False)
                    mm = pe.matmul(featP[:, j % 2, n, 0:HALF], w1b_sb[:, u, 128 * j:128 * (j + 1)], xTb[:, c], start=False, stop=True)
                mm.then_inc(up_done, 1)

            def down(e, u, t, first=False):
                if t == 0:
                    pe.wait_ge(w2_landed[u], (e - u) * 8 + 16)
                    pe.wait_ge(hid_ready, e * FC + FC)
                bank = (u * T + t) % 2
                if first and t < 2:
                    if t == 0:
                        pe.wait_ge(lg_ready, 1)
                else:
                    pe.wait_ge(summed, e * T + t - 1)
                for j in range(FC):
                    mm = pe.matmul(tokP[:, bank, 0:D], hid[:, u, j, 128 * t:128 * (t + 1)], w2_sb[:, u, j, :], start=(j == 0), stop=(j == FC - 1))
                mm.then_inc(down_done, 1)

            def stage(e, u, first=False):
                for j in range(FC):
                    up(e + 1, 1 - u, j)
                    if j >= 1:
                        down(e, u, j - 1, first)

            for j in range(FC):
                up(0, 0, j, True)
            stage(0, 0, True)
            with pe.Fori(1, E // 2) as i:
                stage(i * 2 - 1, 1)
                stage(i * 2, 0)
            for t in range(T):
                down(E - 1, 1, t)

        @block.vector
        def _(dve):
            steps = [0]

            def link(ins):
                steps[0] += 1
                ins.then_inc(dve_step, 1)
                dve.wait_ge(dve_step, steps[0])

            def moments(norm, t, src):
                link(nc.vector.bn_stats(stat[:, norm, t, :], src))
                link(nc.vector.bn_aggr(mv[:, norm, t, :], stat[:, norm, t, :]))
                nc.vector.tensor_scalar(ve[:, norm, t:t + 1], mv[:, norm, t, 1:2], LN_EPS, None, ALU.add).then_inc(ve_ready[norm], 1)

            def normalise(norm, t, src, dst):
                dve.wait_ge(rstd_ready[norm], t + 1)
                nc.vector.tensor_scalar(dst[:, t, :], src[:, t, :], mv[:, norm, t, 0:1], rstd[:, norm, t:t + 1],
                                        ALU.subtract, ALU.mult).then_inc(xn_ready, 1)

            for t in range(T + 1):
                if t < T:
                    dve.wait_ge(h_ready, t + 1)
                    moments(0, t, h[:, t, :])
                if t >= 1:
                    normalise(0, t - 1, h, xn1)

            dve.wait_ge(wa_landed, 16)
            for u in range(2):
                nc.vector.tensor_copy(vm[:, u, :, :, DH:VW].rearrange("p i h v -> p i (h v)"),
                                      wa[0:IT * N, A_MASK:A_MASK + IT].unsqueeze(2).broadcast_to([IT * N, IT, H]))
            for g in range(NG):
                dve.wait_ge(qk_done, g + 1)
                nc.vector.tensor_copy(qa[0:64, g, :].rearrange("p (n t) -> p n t", n=2), featP[0:64, g % 2, :, 0:HALF]).then_inc(q_copied, 1)
                dve.wait_ge(q_copied, g + 1)
                nc.vector.tensor_tensor(qa[64:128, g, :], qa[0:64, g, :], qa[0:64, g, :], ALU.mult).then_inc(q_ready, 1)

            def mask_values(s):
                n = min(IT, B - IT * s)
                rows = n * N
                dve.wait_ge(v_done, s + 1)
                if s >= 2:
                    dve.wait_ge(kv_done, s - 1)
                nc.vector.tensor_tensor(
                    vm[0:rows, s % 2, 0:n, :, 0:DH],
                    tokP[0:rows, s % 2, 0:D].rearrange("p (h d) -> p h d", d=DH).unsqueeze(1).broadcast_to([rows, n, H, DH]),
                    wa[0:rows, A_MASK:A_MASK + n].unsqueeze(2).unsqueeze(3).broadcast_to([rows, n, H, DH]),
                    ALU.mult).then_inc(vm_ready, 1)

            def kv_rows_low(s):
                n = min(IT, B - IT * s)
                dve.wait_ge(kv_done, s + 1)
                nc.vector.tensor_scalar(
                    kv[0:64, IT * s:IT * s + n, :, 0:VW].rearrange("p i h v -> p h i v"),
                    turnP[0:64].rearrange("p b (h c) -> p (b h) c", c=128)[:, 0:PAIRS, 0:2 * VW * n].rearrange("p h (i v) -> p h i v", i=n)[:, :, :, 0:VW],
                    1.0 / M, None, ALU.mult).then_inc(kv_low, 1)

            dve.wait_ge(pool_const, 7)
            for s in range(S):
                mask_values(s)
                if s >= 1:
                    kv_rows_low(s - 1)
            kv_rows_low(S - 1)

            for k in range(4):
                dve.wait_ge(att_done, k + 1)
                both = featP[:, k // 2, k % 2, 0:2 * H * VW].rearrange("p (h v) -> p h v", v=VW)
                link(nc.vector.tensor_scalar(den[:, k, :].unsqueeze(2), both[:, :, DH:VW], DEN_EPS, None, ALU.add))
                link(nc.vector.reciprocal(rden[:, k, :], den[:, k, :]))
                nc.vector.tensor_tensor(o[:, k], both[:, :, 0:DH], rden[:, k, :].unsqueeze(2).broadcast_to([128, 2 * H, DH]),
                                        ALU.mult).then_inc(o_ready, 1)

            dve.wait_ge(wb_landed, 16)
            dve.wait_ge(hb_ready, T)

            def affine(t):
                dve.wait_ge(rstd_ready[1], t + 1)
                link(nc.vector.scalar_tensor_tensor(out=yg[:, t, :], in0=y[:, t, :], scalar=mv[:, 1, t, 0:1], in1=wb[:, B_GAM:B_GAM + D],
                                                    op0=ALU.subtract, op1=ALU.mult))
                link(nc.vector.scalar_tensor_tensor(out=res[:, t, :], in0=yg[:, t, :], scalar=rstd[:, 1, t:t + 1], in1=hb[:, t, :],
                                                    op0=ALU.mult, op1=ALU.add))
                moments(2, t, res[:, t, :])

            for t in range(T + 2):
                if t < T:
                    dve.wait_ge(proj_done, t + 1)
                    nc.vector.tensor_tensor(y[:, t, :], tokP[:, t % 2, 0:D], xn1[:, t, :], ALU.add).then_inc(y_ready, 1)
                    dve.wait_ge(y_ready, t + 1)
                    moments(1, t, y[:, t, :])
                if 1 <= t <= T:
                    affine(t - 1)
                if t >= 2:
                    normalise(2, t - 2, res, xn2)

            dve.wait_ge(router_done, 1)
            logits = tokP[:, 0, 0:T * E].rearrange("p (t e) -> p t e", e=E)
            link(nc.vector.tensor_reduce(lmax[:].unsqueeze(2), logits, AX.X, ALU.max))
            nc.vector.tensor_tensor(lg[:], logits, lmax[:].unsqueeze(2).broadcast_to([128, T, E]), ALU.subtract).then_inc(lg_ready, 1)
            dve.wait_ge(pexp_ready, 1)
            link(nc.vector.tensor_reduce(psumr[:].unsqueeze(2), pe_[:], AX.X, ALU.add))
            link(nc.vector.reciprocal(prec[:], psumr[:]))
            link(nc.vector.tensor_tensor(prob[:], pe_[:], prec[:].unsqueeze(2).broadcast_to([128, T, E]), ALU.mult))
            other = prob[:].unsqueeze(2).broadcast_to([128, T, E, E])
            own = prob[:].unsqueeze(3).broadcast_to([128, T, E, E])
            nc.vector.tensor_tensor(beats[:], other, own, ALU.is_gt)
            link(nc.vector.tensor_tensor(ties[:], other, own, ALU.is_equal))
            earlier = wb[:, B_TRI:B_TRI + E * E].rearrange("p (a b) -> p a b", b=E).unsqueeze(1).broadcast_to([128, T, E, E])
            link(nc.vector.tensor_tensor(ties[:], ties[:], earlier, ALU.mult))
            link(nc.vector.tensor_tensor(beats[:], beats[:], ties[:], ALU.add))
            link(nc.vector.tensor_reduce(rank[:].unsqueeze(3), beats[:], AX.X, ALU.add))
            link(nc.vector.scalar_tensor_tensor(out=gate[:], in0=rank[:], scalar=2.0, in1=prob[:], op0=ALU.is_lt, op1=ALU.mult))

            def add_expert(e, u, t):
                bank = (u * T + t) % 2
                dve.wait_ge(down_done, e * T + t + 1)
                g = gate[:, t, e:e + 1] if isinstance(e, int) else gate[:, t, bass.ds(e, 1)]
                nc.vector.scalar_tensor_tensor(out=res[:, t, :], in0=tokP[:, bank, 0:D], scalar=g, in1=res[:, t, :],
                                               op0=ALU.mult, op1=ALU.add).then_inc(summed, 1)

            for t in range(T):
                add_expert(0, 0, t)
            dve.wait_ge(summed, T)
            for t in range(T):
                add_expert(1, 1, t)
            with dve.Fori(1, E // 2) as i:
                for u in range(2):
                    dve.wait_ge(summed, i * (2 * T) + u * T)
                    for t in range(T):
                        add_expert(i * 2 + u, u, t)


def kernel(x, L0_tok_proj_w, L0_tok_proj_b, L0_tok_cls_token, L0_tok_pos_embedding, L0_attn_W_qkv, L0_attn_W_proj,
           L0_attn_b_proj, L0_attn_gamma, L0_attn_beta, L0_attn_random_features, L0_ffn_router_w, L0_ffn_w1, L0_ffn_w2):
    import concourse.bacc as bacc
    from concourse.bass_utils import run_bass_kernel_spmd

    f32 = np.float32

    def rows(a, n):
        return np.concatenate([a, np.zeros((n - a.shape[0], a.shape[1]), f32)])

    hp = IMG // PATCH
    patches = np.asarray(x).reshape(B, C, hp, PATCH, hp, PATCH).transpose(1, 3, 5, 0, 2, 4).reshape(KC * 128, B, NP)
    xT = np.zeros((KC * 128, TP), f32)
    xT[:, :TOK].reshape(KC * 128, B, N)[:, :, 1:] = patches
    xT = xT.reshape(KC, 128, T, 128).transpose(2, 1, 0, 3).reshape(T, 128, KC * 128)
    embed_w = np.asarray(L0_tok_proj_w).T.reshape(KC, 128, D).transpose(1, 0, 2).reshape(128, KC * D)
    token = np.arange(TP)
    pick = np.zeros((N + 2, TP), f32)
    pick[token[:TOK] % N, token[:TOK]] = 1
    pick[N, :TOK] = token[:TOK] % N == 0
    pick[N + 1, :TOK] = token[:TOK] % N != 0
    pos_w = np.concatenate([np.concatenate([np.asarray(L0_tok_pos_embedding)[0], np.asarray(L0_tok_cls_token)[0],
                                            np.asarray(L0_tok_proj_b)[None]]), pick], axis=1)
    w = np.asarray(L0_attn_W_qkv)
    g = HG * DH
    w_qk = np.concatenate([w[:, D * part + g * i:D * part + g * (i + 1)] for i in range(NG) for part in (0, 1)], axis=1)
    w_v = w[:, 2 * D:]
    rf = np.zeros((128, HG * M), f32)
    for i in range(HG):
        rf[DH * i:DH * (i + 1), M * i:M * (i + 1)] = np.asarray(L0_attn_random_features).T
        rf[64 + DH * i:64 + DH * (i + 1), M * i:M * (i + 1)] = -0.5
    image = np.zeros((128, 4), f32)
    image[np.arange(IT * N), np.arange(IT * N) // N] = 1
    w_p = np.asarray(L0_attn_W_proj)
    w_r = np.asarray(L0_ffn_router_w).T
    wide = [np.broadcast_to(np.asarray(a).reshape(1, -1), (128, a.size))
            for a in (L0_attn_gamma, L0_attn_beta, np.tril(np.ones((E, E), f32), -1))]
    att_a = np.concatenate([w_qk[:128], w_v[:128], rf, image], axis=1)
    att_b = np.concatenate([w_p[:128], w_r[:128], *wide], axis=1)
    att_r = np.concatenate([rows(w_qk[128:], DR + 1), rows(w_v[128:], DR + 1),
                            np.concatenate([w_p[128:], np.asarray(L0_attn_b_proj)[None]]), rows(w_r[128:], DR + 1)], axis=1)
    w1 = np.asarray(L0_ffn_w1)
    w2 = np.asarray(L0_ffn_w2).reshape(E, FC, 128, D).transpose(0, 2, 1, 3)

    nc = bacc.Bacc("TRN2", target_bir_lowering=False, num_devices=1)
    arrays, args = {}, []
    for name, a in (("xT", xT), ("embed_w", embed_w), ("pos_w", pos_w), ("ident_w", np.eye(128, dtype=f32)), ("att_a", att_a),
                    ("att_b", att_b), ("att_r", att_r), ("w1a", w1[:, :128]), ("w1b", w1[:, 128:]), ("w2", w2)):
        arrays[name] = np.ascontiguousarray(a)
        args.append(nc.dram_tensor(name, a.shape, F32, kind="ExternalInput").ap())
    args.append(nc.dram_tensor("out", (TOK, D), F32, kind="ExternalOutput").ap())
    vit_tower(nc, *args)
    r = run_bass_kernel_spmd(nc, [arrays], core_ids=[0])
    return r.results[0]["out"].reshape(B, N, D)
```

```python
from contextlib import ExitStack

import numpy as np

import concourse.bass as bass
from concourse import mybir
from concourse.alu_op_type import AluOpType as ALU

ACT = mybir.ActivationFunctionType
AX = mybir.AxisListType
F32 = mybir.dt.float32
F32R = mybir.dt.float32r

B, C, IMG, PATCH = 16, 3, 96, 16
NP = (IMG // PATCH) ** 2
N = NP + 1
TOK = B * N
HALF = TOK // 2
D = 192
DR = D - 128
KC = PATCH * PATCH * C // 128
T = -(-TOK // 128)
TP = 128 * T
LAST = TOK - 128 * (T - 1)
H, DH, M = 12, 16, 64
PAIRS = H // 2
HG = 4
NG = H // HG
IT = 3
S = -(-B // IT)
VW = DH + 1
E, F = 8, 768
FC = F // 128
WB = 2 * 128 + D
LN_EPS = 1e-5
DEN_EPS = 1e-6

A_QK, A_V, A_RF, A_MASK = 0, NG * 128, NG * 128 + D, NG * 128 + D + HG * M
A_END = A_MASK + 4
B_P, B_R, B_GAM, B_BET, B_TRI = 0, D, D + E, 2 * D + E, 3 * D + E
B_END = B_TRI + E * E
R_QK, R_V, R_P, R_R = 0, NG * 128, NG * 128 + D, NG * 128 + 2 * D
R_END = R_R + E


def vit_tower(nc, xT, embed_w, pos_w, ident_w, att_a, att_b, att_r, expert_w, out):
    ctx = ExitStack()
    with ctx:
        def sb(name, shape, dt=F32):
            return ctx.enter_context(nc.sbuf_tensor(name, shape, dt))

        def psum(name, shape):
            return ctx.enter_context(nc.psum_tensor(name, shape, F32))

        def sem(name):
            return ctx.enter_context(nc.semaphore(name))

        tokP = psum("tokP", [128, 2, 512])
        turnP = psum("turnP", [128, 2, 512])
        featP = psum("featP", [128, 2, 2, 512])

        ident = sb("ident", [128, 128])
        wa = sb("wa", [128, A_END])
        wb = sb("wb", [128, B_END])
        wr = sb("wr", [DR + 1, R_END])

        h = sb("h", [128, T, D])
        hb = sb("hb", [128, T, D])
        xn1 = sb("xn1", [128, T, D])
        xTa = sb("xTa", [128, TP])
        xTb = sb("xTb", [DR, TP])
        nmr = sb("nmr", [128, T])
        stat = sb("stat", [128, 3, T, 6])
        mv = sb("mv", [128, 3, T, 2])
        ve = sb("ve", [128, 3, T])
        rstd = sb("rstd", [128, 3, T])
        mhalf = sb("mhalf", [128, 1])
        den = sb("den", [128, 4, 2 * H])
        rden = sb("rden", [128, 4, 2 * H])
        oTa = sb("oTa", [128, TP])
        oTb = sb("oTb", [DR + 1, TP])
        res = sb("res", [128, T, D])
        xn2 = sb("xn2", [128, T, 256])
        lmax = sb("lmax", [128, T])
        lg = sb("lg", [128, T, E])
        pe_ = sb("pexp", [128, T, E])
        psumr = sb("psumr", [128, T])
        prec = sb("prec", [128, T])
        prob = sb("prob", [128, T, E])
        beats = sb("beats", [128, T, E, E])
        ties = sb("ties", [128, T, E, E])
        rank = sb("rank", [128, T, E])
        gate = sb("gate", [128, T, E])
        x2 = sb("x2", [128, 2, TP])
        x2h = sb("x2h", [128, 2, TP], F32R)
        x2l = sb("x2l", [128, TP], F32R)
        w_raw = sb("w_raw", [128, 2, FC, WB])
        whl = sb("whl", [128, 2, FC, 2, WB], F32R)
        wh, wl = whl[:, :, :, 0, :], whl[:, :, :, 1, :]

        attention = ExitStack()

        def early_sb(name, shape):
            return attention.enter_context(nc.sbuf_tensor(name, shape, F32))

        with ExitStack() as embedding:
            x_sb = embedding.enter_context(nc.sbuf_tensor("x_sb", [128, T, KC * 128], F32))
            embed_sb = embedding.enter_context(nc.sbuf_tensor("embed_sb", [128, KC, D], F32))
            pos_sb = embedding.enter_context(nc.sbuf_tensor("pos_sb", [N + 2, D + TP], F32))
        qp = early_sb("qp", [128, PAIRS, TOK])
        qa = early_sb("qa", [128, NG, TOK])
        ka = early_sb("ka", [128, NG, TOK])
        kp = early_sb("kp", [IT * N, 2, H * M])
        vm = early_sb("vm", [IT * N, 2, IT, H, VW])
        kv = early_sb("kv", [128, B, PAIRS, 2 * VW])
        o = early_sb("o", [128, 4, 2 * H, DH])
        attention.close()
        act_full = sb("act_full", [128, 2, TOK])
        res_low = sb("res_low", [128, T, D])
        hh = sb("hh", [128, 2, FC, TOK], F32R)
        hl = sb("hl", [128, 2, FC, TOK], F32R)

        x_landed = [sem(f"x_landed{t}") for t in range(T)]
        embed_landed = sem("embed_landed")
        pos_landed = sem("pos_landed")
        ident_landed = sem("ident_landed")
        wa_landed = sem("wa_landed")
        wb_landed = sem("wb_landed")
        wr_landed = sem("wr_landed")
        w_landed = [sem(f"w_landed{u}") for u in range(2)]
        w_high = sem("w_high")
        w_split = sem("w_split")
        x2_high = sem("x2_high")
        x2_split = sem("x2_split")
        hid_split = sem("hid_split")
        out_stored = sem("out_stored")
        pool_const = sem("pool_const")
        embed_done = sem("embed_done")
        h_ready = sem("h_ready")
        ve_ready = [sem(f"ve_ready{n}") for n in range(3)]
        rstd_ready = [sem(f"rstd_ready{n}") for n in range(3)]
        hb_ready = sem("hb_ready")
        xn_ready = sem("xn_ready")
        turned = sem("turned")
        xT_ready = sem("xT_ready")
        x2_ready = sem("x2_ready")
        qk_done = sem("qk_done")
        q_copied = sem("q_copied")
        k_copied = sem("k_copied")
        q_ready = sem("q_ready")
        k_ready = sem("k_ready")
        v_done = sem("v_done")
        vm_ready = sem("vm_ready")
        kproj_done = sem("kproj_done")
        qproj_done = sem("qproj_done")
        kp_ready = sem("kp_ready")
        qp_ready = sem("qp_ready")
        kv_done = sem("kv_done")
        kv_low = sem("kv_low")
        kv_high = sem("kv_high")
        att_done = sem("att_done")
        bank_cleared = sem("bank_cleared")
        nmr_ready = sem("nmr_ready")
        xn2_ready = sem("xn2_ready")
        y_done = sem("y_done")
        o_ready = sem("o_ready")
        o_turned = sem("o_turned")
        oT_ready = sem("oT_ready")
        router_done = sem("router_done")
        lg_ready = sem("lg_ready")
        pexp_ready = sem("pexp_ready")
        up_done = sem("up_done")
        hid_ready = sem("hid_ready")
        down_done = sem("down_done")
        summed = sem("summed")
        res_ready = sem("res_ready")
        dve_step = sem("dve_step")

        def y_tile(t):
            return featP[:, t // 2, t % 2, 0:D] if t < 4 else tokP[:, 1, 0:D]

        block = ctx.enter_context(nc.Block())

        @block.sync
        def _(sp):
            sp.dma_start(embed_sb[:].rearrange("p c d -> p (c d)"), embed_w).then_inc(embed_landed, 16)
            sp.dma_start(x_sb[:, 0, :], xT[0]).then_inc(x_landed[0], 16)
            sp.dma_start(pos_sb[:], pos_w).then_inc(pos_landed, 16)
            sp.dma_start(x_sb[:, 1, :], xT[1]).then_inc(x_landed[1], 16)
            sp.dma_start(ident[:], ident_w).then_inc(ident_landed, 16)
            sp.dma_start(x_sb[:, 2, :], xT[2]).then_inc(x_landed[2], 16)
            sp.dma_start(x_sb[:, 3, :], xT[3]).then_inc(x_landed[3], 16)
            sp.dma_start(wr[:], att_r).then_inc(wr_landed, 16)
            sp.dma_start(x_sb[:, 4, :], xT[4]).then_inc(x_landed[4], 16)
            sp.dma_start(wa[:], att_a).then_inc(wa_landed, 16)
            sp.dma_start(wb[:], att_b).then_inc(wb_landed, 16)
            for k in range(2):
                sp.dma_start(w_raw[:, k].rearrange("p c w -> p (c w)"), expert_w[k]).then_inc(w_landed[k], 16)

            def load(k, u):
                sp.wait_ge(w_split, (k - 1) * FC)
                src = expert_w[k] if isinstance(k, int) else expert_w[bass.ds(k, 1)].rearrange("k p w -> (k p) w")
                sp.dma_start(w_raw[:, u].rearrange("p c w -> p (c w)"), src).then_inc(w_landed[u], 16)

            with sp.Fori(1, E // 2) as i:
                load(i * 2, 0)
                load(i * 2 + 1, 1)
            load(E, 0)
            for t in range(T):
                n = 128 if t < T - 1 else LAST
                sp.wait_ge(res_ready, t + 1)
                sp.dma_start(out[128 * t:128 * t + n, :], res[0:n, t, :]).then_inc(out_stored, 16)
            sp.wait_ge(out_stored, 16 * T)

        @block.gpsimd
        def _(pool):
            nc.gpsimd.memset(mhalf[:], -0.5).then_inc(pool_const, 1)
            nc.gpsimd.memset(kv[:], 0.0).then_inc(pool_const, 1)
            nc.gpsimd.memset(oTa[:, TOK:TP], 0.0).then_inc(pool_const, 1)
            nc.gpsimd.memset(oTb[0:DR, TOK:TP], 0.0).then_inc(pool_const, 1)
            pool.wait_ge(pool_const, 4)
            nc.gpsimd.memset(oTb[DR:DR + 1, :], 1.0).then_inc(pool_const, 1)
            pool.wait_ge(pool_const, 5)

            def inverse_root(norm, t):
                pool.wait_ge(ve_ready[norm], t + 1)
                nc.gpsimd.tensor_tensor(rstd[:, norm, t:t + 1], ve[:, norm, t:t + 1], mhalf[:], ALU.pow).then_inc(rstd_ready[norm], 1)

            for t in range(T):
                inverse_root(0, t)
            pool.wait_ge(wb_landed, 16)
            for t in range(T):
                nc.gpsimd.tensor_tensor(hb[:, t, :], h[:, t, :], wb[:, B_BET:B_BET + D], ALU.add).then_inc(hb_ready, 1)
            for t in range(T + 1):
                if t < T:
                    inverse_root(1, t)
                if t >= 1:
                    inverse_root(2, t - 1)

        @block.scalar
        def _(act):
            for t in range(T + 1):
                if t < T:
                    act.wait_ge(embed_done, t + 1)
                    nc.scalar.copy(h[:, t, :], tokP[:, t % 2, 0:D]).then_inc(h_ready, 1)
                if t >= 1:
                    act.wait_ge(turned, t)
                    c = slice(128 * (t - 1), 128 * t)
                    nc.scalar.copy(xTa[:, c], turnP[:, (t - 1) % 2, 0:128]).then_inc(xT_ready, 1)
                    nc.scalar.copy(xTb[:, c], turnP[0:DR, (t - 1) % 2, 128:256]).then_inc(xT_ready, 1)
            for i in range(2 * NG):
                n, g = i // NG, i % NG
                c = slice(HALF * n, HALF * (n + 1))
                act.wait_ge(qk_done, i + 1)
                nc.scalar.copy(ka[0:64, g, c], featP[64:128, (i // 2) % 2, i % 2, 0:HALF]).then_inc(k_copied, 1)
                act.wait_ge(k_copied, i + 1)
                nc.scalar.activation(ka[64:128, g, c], ka[0:64, g, c], ACT.Square).then_inc(k_ready, 1)

            def kv_rows_high(s):
                n = min(IT, B - IT * s)
                act.wait_ge(kv_done, s + 1)
                nc.scalar.activation(
                    kv[64:128, IT * s:IT * s + n, :, VW:2 * VW].rearrange("p i h v -> p h i v"),
                    turnP[64:128].rearrange("p b (h c) -> p (b h) c", c=128)[:, 0:PAIRS, 0:2 * VW * n].rearrange("p h (i v) -> p h i v", i=n)[:, :, :, VW:2 * VW],
                    ACT.Copy, scale=1.0 / M).then_inc(kv_high, 1)

            def high(k, u, j, cols=slice(0, WB)):
                nc.scalar.copy(wh[:, u, j, cols], w_raw[:, u, j, cols]).then_inc(w_high, 1)

            act.wait_ge(pool_const, 5)
            act.wait_ge(w_landed[0], 16)
            act.wait_ge(w_landed[1], 16)
            for s in range(S):
                rows = min(IT, B - IT * s) * N
                act.wait_ge(kproj_done, s + 1)
                if s >= 2:
                    act.wait_ge(kv_done, s - 1)
                nc.scalar.activation(kp[0:rows, s % 2, :], featP[0:rows, 0].rearrange("p b c -> p (b c)")[:, 0:H * M], ACT.Exp).then_inc(kp_ready, 1)
                act.wait_ge(qproj_done, s + 1)
                nc.scalar.activation(qp[:, s, :].rearrange("p (n t) -> p n t", n=2), featP[:, 1, :, 0:HALF], ACT.Exp).then_inc(qp_ready, 1)
                if s >= 1:
                    kv_rows_high(s - 1)
                high(0, 0, s, slice(0, 256))
            kv_rows_high(S - 1)
            def take_oT(k):
                act.wait_ge(o_turned, k + 1)
                c = slice(4 * N * k, 4 * N * (k + 1))
                for dst, at, rows in ((oTa, 0, 128), (oTb, 256, DR)):
                    nc.scalar.copy(dst[0:rows, c].rearrange("p (i n) -> p i n", n=N),
                                   turnP[0:rows, k % 2, at:at + 256].rearrange("p (i n) -> p i n", n=64)[:, :, 0:N]).then_inc(oT_ready, 1)

            for j in range(FC):
                high(1, 1, j)
            for k in range(4):
                take_oT(k)

            for t in range(T + 1):
                if t < T:
                    act.wait_ge(nmr_ready, t + 1)
                    nc.scalar.activation(xn2[:, t, 0:D], res[:, t, :], ACT.Identity, bias=nmr[:, t:t + 1],
                                         scale=rstd[:, 2, t:t + 1]).then_inc(xn2_ready, 1)
                    nc.scalar.activation(xn2[:, t, D:256], res[:, t, 128:D], ACT.Identity, bias=nmr[:, t:t + 1],
                                         scale=rstd[:, 2, t:t + 1]).then_inc(xn2_ready, 1)
                if t >= 1:
                    act.wait_ge(turned, T + t)
                    c = slice(128 * (t - 1), 128 * t)
                    src = turnP[:, (t - 1) % 2, 0:256].rearrange("p (h n) -> p h n", h=2)
                    nc.scalar.copy(x2h[:, :, c], src).then_inc(x2_high, 1)
                    nc.scalar.copy(x2[:, :, c], src).then_inc(x2_ready, 1)
            act.wait_ge(lg_ready, 1)
            nc.scalar.activation(pe_[:], lg[:], ACT.Exp).then_inc(pexp_ready, 1)

            def gelu(e, u, j, first=False):
                act.wait_ge(up_done, e * FC + j + 1)
                src = featP[:, j % 2, :, 0:HALF]
                nc.scalar.activation(hh[:, u, j, 0:TOK].rearrange("p (n t) -> p n t", n=2), src, ACT.Gelu_apprx_tanh)
                if not (first and j < 2):
                    act.wait_ge(hid_split, e * FC + j - 1)
                nc.scalar.activation(act_full[:, j % 2, :].rearrange("p (n t) -> p n t", n=2), src,
                                     ACT.Gelu_apprx_tanh).then_inc(hid_ready, 1)

            def stage(e, u, first=False):
                act.wait_ge(w_landed[u], (e - u) * 8 + 32)
                act.wait_ge(up_done if first else down_done, FC if first else e * T)
                for j in range(FC):
                    high(e + 2, u, j)
                    gelu(e + 1, 1 - u, j)

            for j in range(FC):
                gelu(0, 0, j, True)
            stage(0, 0, True)
            with act.Fori(1, E // 2) as i:
                stage(i * 2 - 1, 1)
                stage(i * 2, 0)

        @block.tensor
        def _(pe):
            def turn(t):
                pe.wait_ge(xn_ready, t + 1)
                if t >= 2:
                    pe.wait_ge(xT_ready, 2 * (t - 1))
                pe.transpose(turnP[:, t % 2, 0:128], xn1[:, t, 0:128], ident[:])
                pe.transpose(turnP[0:DR, t % 2, 128:256], xn1[:, t, 128:D], ident[:]).then_inc(turned, 1)

            pe.wait_ge(embed_landed, 16)
            for t in range(T):
                if t < T:
                    pe.wait_ge(x_landed[t], 16)
                    if t >= 2:
                        pe.wait_ge(h_ready, t - 1)
                    for c in range(KC):
                        pe.matmul(tokP[:, t % 2, 0:D], x_sb[:, t, 128 * c:128 * (c + 1)], embed_sb[:, c, :], start=(c == 0), stop=False)
                    if t == 0:
                        pe.wait_ge(pos_landed, 16)
                    pe.matmul(tokP[:, t % 2, 0:D], pos_sb[:, D + 128 * t:D + 128 * (t + 1)], pos_sb[:, 0:D], start=False, stop=True).then_inc(embed_done, 1)
                if t == 2:
                    pe.wait_ge(ident_landed, 16)
                if t >= 2:
                    turn(t - 2)

            pe.wait_ge(wa_landed, 16)
            pe.wait_ge(wr_landed, 16)
            for i in range(2 * NG):
                n, g = i // NG, i % NG
                if i in (1, 2):
                    turn(T - 3 + i)
                pe.wait_ge(xT_ready, 2 * (3 if n == 0 else T))
                if i >= 4:
                    pe.wait_ge(q_copied, i - 3)
                    pe.wait_ge(k_copied, i - 3)
                c = slice(HALF * n, HALF * (n + 1))
                bank = featP[:, (i // 2) % 2, i % 2, 0:HALF]
                pe.matmul(bank, wa[:, A_QK + 128 * g:A_QK + 128 * (g + 1)], xTa[:, c], start=True, stop=False)
                pe.matmul(bank, wr[0:DR, R_QK + 128 * g:R_QK + 128 * (g + 1)], xTb[:, c], start=False, stop=True).then_inc(qk_done, 1)

            def key_sums(s):
                n = min(IT, B - IT * s)
                pe.wait_ge(kp_ready, s + 1)
                pe.wait_ge(vm_ready, s + 1)
                if s >= 1:
                    pe.wait_ge(kv_low, s)
                    pe.wait_ge(kv_high, s)
                for p in range(PAIRS):
                    mm = pe.matmul(turnP[:, p // 4, 128 * (p % 4):128 * (p % 4) + 2 * VW * n].rearrange("p (i v) -> p i v", i=n),
                                   kp[0:n * N, s % 2, 128 * p:128 * (p + 1)],
                                   vm[0:n * N, s % 2, 0:n, 2 * p:2 * p + 2, :].rearrange("p i h v -> p i (h v)"), start=True, stop=True)
                mm.then_inc(kv_done, 1)

            def values(s):
                rows = min(IT, B - IT * s) * N
                c = slice(IT * N * s, IT * N * s + rows)
                if s >= 2:
                    pe.wait_ge(vm_ready, s - 1)
                pe.matmul(tokP[0:rows, s % 2, 0:D], xTa[:, c], wa[:, A_V:A_V + D], start=True, stop=False)
                pe.matmul(tokP[0:rows, s % 2, 0:D], xTb[:, c], wr[0:DR, R_V:R_V + D], start=False, stop=True).then_inc(v_done, 1)

            values(0)
            values(1)
            for s in range(S):
                rows = min(IT, B - IT * s) * N
                c = slice(IT * N * s, IT * N * s + rows)
                if s == 0:
                    pe.wait_ge(k_ready, 2 * NG)
                    pe.wait_ge(q_ready, 2 * NG)
                else:
                    pe.wait_ge(kp_ready, s)
                for g in range(NG):
                    mm = pe.matmul(featP[0:rows, 0, g // 2, 256 * (g % 2):256 * (g % 2) + HG * M], ka[:, g, c], wa[:, A_RF:A_RF + HG * M], start=True, stop=True)
                mm.then_inc(kproj_done, 1)
                if s >= 1:
                    pe.wait_ge(qp_ready, s)
                for n in range(2):
                    mm = pe.matmul(featP[:, 1, n, 0:HALF], wa[:, A_RF + 128 * (s % 2):A_RF + 128 * (s % 2 + 1)],
                                   qa[:, s // 2, HALF * n:HALF * (n + 1)], start=True, stop=True)
                mm.then_inc(qproj_done, 1)
                if s >= 1:
                    key_sums(s - 1)
                if s + 2 < S:
                    values(s + 2)
            key_sums(S - 1)

            pe.wait_ge(qp_ready, S)
            pe.wait_ge(kv_low, S)
            pe.wait_ge(kv_high, S)
            pe.wait_ge(bank_cleared, 1)

            def turn_o(k):
                pe.wait_ge(o_ready, k + 1)
                if k >= 2:
                    pe.wait_ge(oT_ready, 2 * (k - 1))
                for gg in range(2):
                    f = o[:, k, H * gg:H * (gg + 1), :].rearrange("p h d -> p (h d)")
                    pe.transpose(turnP[:, k % 2, 128 * gg:128 * (gg + 1)], f[:, 0:128], ident[:])
                    mm = pe.transpose(turnP[0:DR, k % 2, 256 + 128 * gg:256 + 128 * (gg + 1)], f[:, 128:D], ident[:])
                mm.then_inc(o_turned, 1)

            for k in range(4):
                for gg in range(2):
                    for half in range(2):
                        b = 4 * k + 2 * gg + half
                        for p in range(PAIRS):
                            at = 2 * VW * (PAIRS * gg + p)
                            mm = pe.matmul(featP[64 * half:64 * half + N, k // 2, k % 2, at:at + 2 * VW],
                                           qp[:, p, N * b:N * (b + 1)], kv[:, b, p, :], start=True, stop=True)
                mm.then_inc(att_done, 1)
                if k >= 1:
                    turn_o(k - 1)
            turn_o(3)

            pe.wait_ge(wb_landed, 16)
            for t in range(T):
                pe.wait_ge(oT_ready, 2 * (-(-min(128 * (t + 1), TOK) // (4 * N))))
                c = slice(128 * t, 128 * (t + 1))
                y = y_tile(t)
                pe.matmul(y, ident[:], xn1[:, t, :], start=True, stop=False)
                pe.matmul(y, oTa[:, c], wb[:, B_P:B_P + D], start=False, stop=False)
                pe.matmul(y, oTb[:, c], wr[:, R_P:R_P + D], start=False, stop=True).then_inc(y_done, 1)

            for t in range(T + 1):
                if t < T:
                    pe.wait_ge(xn2_ready, 2 * (t + 1))
                    if t >= 2:
                        pe.wait_ge(x2_ready, t - 1)
                    pe.transpose(turnP[:, t % 2, 0:128], xn2[:, t, 0:128], ident[:])
                    pe.transpose(turnP[:, t % 2, 128:256], xn2[:, t, 128:256], ident[:]).then_inc(turned, 1)
                if t >= 1:
                    pe.wait_ge(x2_ready, t)
                    c = slice(128 * (t - 1), 128 * t)
                    logits = tokP[:, 0, E * (t - 1):E * t]
                    pe.matmul(logits, x2[:, 0, c], wb[:, B_R:B_R + E], start=True, stop=False)
                    pe.matmul(logits, x2[0:DR, 1, c], wr[0:DR, R_R:R_R + E], start=False, stop=True).then_inc(router_done, 1)

            def up(e, u, j, first=False):
                pe.wait_ge(w_split, e * FC + j + 1)
                if not (first and j < 2):
                    pe.wait_ge(hid_ready, e * FC + j - 1)
                a, b = slice(0, 128), slice(128, 256)
                terms = [(wh[:, u, j, a], x2h[:, 0]), (wh[:, u, j, a], x2l[:]), (wl[:, u, j, a], x2h[:, 0]),
                         (wh[:, u, j, b], x2h[:, 1]),
                         (wl[0:DR, u, j, b], x2h[0:DR, 1])]
                for k, (weights, x) in enumerate(terms):
                    for n in range(2):
                        mm = pe.matmul(featP[:, j % 2, n, 0:HALF], weights, x[:, HALF * n:HALF * (n + 1)],
                                       start=(k == 0), stop=(k == len(terms) - 1))
                mm.then_inc(up_done, 1)

            def down(e, u, t, first=False):
                if t == 0:
                    pe.wait_ge(w_split, e * FC + 2 * FC)
                    pe.wait_ge(hid_split, e * FC + FC)
                bank = (u * T + t) % 2
                if first and t < 2:
                    if t == 0:
                        pe.wait_ge(lg_ready, 1)
                else:
                    pe.wait_ge(summed, e * T + t - 1)
                n = 128 if t < T - 1 else LAST
                c = slice(128 * t, 128 * t + n)
                w = slice(256, WB)
                for j in range(FC):
                    pe.matmul(tokP[0:n, bank, 0:2 * D].rearrange("p (k d) -> p k d", k=2), hh[:, u, j, c], whl[:, 1 - u, j, :, w],
                              start=(j == 0), stop=(j == FC - 1), skip_group_check=True)
                    mm = pe.matmul(tokP[0:n, bank, 0:D], hl[:, u, j, c], wh[:, 1 - u, j, w], start=False, stop=(j == FC - 1), skip_group_check=True)
                mm.then_inc(down_done, 1)

            def stage(e, u, first=False):
                for j in range(FC):
                    up(e + 1, 1 - u, j)
                    if j >= 1:
                        down(e, u, j - 1, first)

            pe.wait_ge(x2_split, T)
            for j in range(FC):
                up(0, 0, j, True)
            stage(0, 0, True)
            with pe.Fori(1, E // 2) as i:
                stage(i * 2 - 1, 1)
                stage(i * 2, 0)
            for t in range(T):
                down(E - 1, 1, t)

        @block.vector
        def _(dve):
            steps = [0]

            def mark(ins):
                steps[0] += 1
                ins.then_inc(dve_step, 1)
                return steps[0]

            def link(ins):
                dve.wait_ge(dve_step, mark(ins))

            def moments(norm, t, src):
                link(nc.vector.bn_stats(stat[:, norm, t, :], src))
                link(nc.vector.bn_aggr(mv[:, norm, t, :], stat[:, norm, t, :]))
                add_eps(norm, t)

            def add_eps(norm, t):
                nc.vector.tensor_scalar(ve[:, norm, t:t + 1], mv[:, norm, t, 1:2], LN_EPS, None, ALU.add).then_inc(ve_ready[norm], 1)

            def normalise(norm, t, src, dst):
                dve.wait_ge(rstd_ready[norm], t + 1)
                nc.vector.tensor_scalar(dst[:, t, :], src[:, t, :], mv[:, norm, t, 0:1], rstd[:, norm, t:t + 1],
                                        ALU.subtract, ALU.mult).then_inc(xn_ready, 1)

            nc.vector.memset(featP[:, :, :, HALF:2 * H * VW], 0.0).then_inc(bank_cleared, 1)
            for t in range(T + 1):
                if t < T:
                    dve.wait_ge(h_ready, t + 1)
                    moments(0, t, h[:, t, :])
                if t >= 1:
                    normalise(0, t - 1, h, xn1)

            dve.wait_ge(wa_landed, 16)
            for u in range(2):
                nc.vector.tensor_copy(vm[:, u, :, :, DH:VW].rearrange("p i h v -> p i (h v)"),
                                      wa[0:IT * N, A_MASK:A_MASK + IT].unsqueeze(2).broadcast_to([IT * N, IT, H]))
            for i in range(2 * NG):
                n, g = i // NG, i % NG
                c = slice(HALF * n, HALF * (n + 1))
                dve.wait_ge(qk_done, i + 1)
                nc.vector.tensor_copy(qa[0:64, g, c], featP[0:64, (i // 2) % 2, i % 2, 0:HALF]).then_inc(q_copied, 1)
                dve.wait_ge(q_copied, i + 1)
                nc.vector.tensor_tensor(qa[64:128, g, c], qa[0:64, g, c], qa[0:64, g, c], ALU.mult).then_inc(q_ready, 1)

            def mask_values(s):
                n = min(IT, B - IT * s)
                rows = n * N
                dve.wait_ge(v_done, s + 1)
                if s >= 2:
                    dve.wait_ge(kv_done, s - 1)
                nc.vector.tensor_tensor(
                    vm[0:rows, s % 2, 0:n, :, 0:DH],
                    tokP[0:rows, s % 2, 0:D].rearrange("p (h d) -> p h d", d=DH).unsqueeze(1).broadcast_to([rows, n, H, DH]),
                    wa[0:rows, A_MASK:A_MASK + n].unsqueeze(2).unsqueeze(3).broadcast_to([rows, n, H, DH]),
                    ALU.mult).then_inc(vm_ready, 1)

            def kv_rows_low(s):
                n = min(IT, B - IT * s)
                dve.wait_ge(kv_done, s + 1)
                nc.vector.tensor_scalar(
                    kv[0:64, IT * s:IT * s + n, :, 0:VW].rearrange("p i h v -> p h i v"),
                    turnP[0:64].rearrange("p b (h c) -> p (b h) c", c=128)[:, 0:PAIRS, 0:2 * VW * n].rearrange("p h (i v) -> p h i v", i=n)[:, :, :, 0:VW],
                    1.0 / M, None, ALU.mult).then_inc(kv_low, 1)

            def low(k, u, j, cols=slice(0, WB)):
                dve.wait_ge(w_high, k * FC + j + 1)
                nc.vector.tensor_tensor(wl[:, u, j, cols], w_raw[:, u, j, cols], wh[:, u, j, cols].bitcast(F32), ALU.subtract).then_inc(w_split, 1)

            dve.wait_ge(pool_const, 5)
            for s in range(S):
                mask_values(s)
                if s >= 1:
                    kv_rows_low(s - 1)
                    low(0, 0, s - 1, slice(0, 256))
            kv_rows_low(S - 1)
            low(0, 0, S - 1, slice(0, 256))

            for k in range(4):
                dve.wait_ge(att_done, k + 1)
                both = featP[:, k // 2, k % 2, 0:2 * H * VW].rearrange("p (h v) -> p h v", v=VW)
                link(nc.vector.tensor_scalar(den[:, k, :].unsqueeze(2), both[:, :, DH:VW], DEN_EPS, None, ALU.add))
                link(nc.vector.reciprocal(rden[:, k, :], den[:, k, :]))
                nc.vector.tensor_tensor(o[:, k], both[:, :, 0:DH], rden[:, k, :].unsqueeze(2).broadcast_to([128, 2 * H, DH]),
                                        ALU.mult).then_inc(o_ready, 1)
                low(1, 1, k)

            dve.wait_ge(wb_landed, 16)
            dve.wait_ge(hb_ready, T)

            def x2_low(t):
                c = slice(128 * t, 128 * (t + 1))
                dve.wait_ge(x2_ready, t + 1)
                nc.vector.tensor_tensor(x2l[:, c], x2[:, 0, c], x2h[:, 0, c].bitcast(F32), ALU.subtract)
                nc.vector.tensor_tensor(x2h[64:128, 1, c], x2[64:128, 1, c], x2h[64:128, 1, c].bitcast(F32), ALU.subtract).then_inc(x2_split, 1)

            mark_of = {}

            def need(*what):
                dve.wait_ge(dve_step, mark_of[what])

            for t in range(T + 2):
                a, b, c = t, t - 1, t - 2
                if a < T:
                    dve.wait_ge(y_done, a + 1)
                    mark_of["stats1", a] = mark(nc.vector.bn_stats(stat[:, 1, a, :], y_tile(a)))
                if 0 <= b < T:
                    dve.wait_ge(rstd_ready[1], b + 1)
                    mark_of["affine", b] = mark(nc.vector.scalar_tensor_tensor(
                        out=res[:, b, :], in0=y_tile(b), scalar=mv[:, 1, b, 0:1], in1=wb[:, B_GAM:B_GAM + D], op0=ALU.subtract, op1=ALU.mult))
                if a < T:
                    need("stats1", a)
                    mark_of["mean1", a] = mark(nc.vector.bn_aggr(mv[:, 1, a, :], stat[:, 1, a, :]))
                if 0 <= b < T:
                    need("affine", b)
                    mark_of["residual", b] = mark(nc.vector.scalar_tensor_tensor(
                        out=res[:, b, :], in0=res[:, b, :], scalar=rstd[:, 1, b:b + 1], in1=hb[:, b, :], op0=ALU.mult, op1=ALU.add))
                if a < T:
                    need("mean1", a)
                    add_eps(1, a)
                if 0 <= c < T:
                    dve.wait_ge(rstd_ready[2], c + 1)
                    nc.vector.scalar_tensor_tensor(out=nmr[:, c:c + 1], in0=mv[:, 2, c, 0:1], scalar=-1.0, in1=rstd[:, 2, c:c + 1],
                                                   op0=ALU.mult, op1=ALU.mult).then_inc(nmr_ready, 1)
                if 0 <= b < T:
                    need("residual", b)
                    mark_of["stats2", b] = mark(nc.vector.bn_stats(stat[:, 2, b, :], res[:, b, :]))
                if 0 <= b < T:
                    need("stats2", b)
                    mark_of["mean2", b] = mark(nc.vector.bn_aggr(mv[:, 2, b, :], stat[:, 2, b, :]))
                    need("mean2", b)
                    add_eps(2, b)
            for j in (4, 5):
                low(1, 1, j)
            for t in range(T):
                x2_low(t)

            def hidden_low(e, u, j):
                dve.wait_ge(hid_ready, e * FC + j + 1)
                nc.vector.tensor_tensor(hl[:, u, j, 0:TOK], act_full[:, j % 2, :], hh[:, u, j, 0:TOK].bitcast(F32), ALU.subtract).then_inc(hid_split, 1)

            dve.wait_ge(router_done, T)
            logits = tokP[:, 0, 0:T * E].rearrange("p (t e) -> p t e", e=E)
            link(nc.vector.tensor_reduce(lmax[:].unsqueeze(2), logits, AX.X, ALU.max))
            nc.vector.tensor_tensor(lg[:], logits, lmax[:].unsqueeze(2).broadcast_to([128, T, E]), ALU.subtract).then_inc(lg_ready, 1)
            hidden_low(0, 0, 0)
            dve.wait_ge(pexp_ready, 1)
            link(nc.vector.tensor_reduce(psumr[:].unsqueeze(2), pe_[:], AX.X, ALU.add))
            link(nc.vector.reciprocal(prec[:], psumr[:]))
            link(nc.vector.tensor_tensor(prob[:], pe_[:], prec[:].unsqueeze(2).broadcast_to([128, T, E]), ALU.mult))
            hidden_low(0, 0, 1)
            other = prob[:].unsqueeze(2).broadcast_to([128, T, E, E])
            own = prob[:].unsqueeze(3).broadcast_to([128, T, E, E])
            nc.vector.tensor_tensor(beats[:], other, own, ALU.is_gt)
            link(nc.vector.tensor_tensor(ties[:], other, own, ALU.is_equal))
            hidden_low(0, 0, 2)
            earlier = wb[:, B_TRI:B_TRI + E * E].rearrange("p (a b) -> p a b", b=E).unsqueeze(1).broadcast_to([128, T, E, E])
            link(nc.vector.tensor_tensor(ties[:], ties[:], earlier, ALU.mult))
            hidden_low(0, 0, 3)
            link(nc.vector.tensor_tensor(beats[:], beats[:], ties[:], ALU.add))
            hidden_low(0, 0, 4)
            link(nc.vector.tensor_reduce(rank[:].unsqueeze(3), beats[:], AX.X, ALU.add))
            link(nc.vector.scalar_tensor_tensor(out=gate[:], in0=rank[:], scalar=2.0, in1=prob[:], op0=ALU.is_lt, op1=ALU.mult))
            hidden_low(0, 0, 5)

            def add_expert(e, u, t, first=False):
                bank = (u * T + t) % 2
                dve.wait_ge(down_done, e * T + t + 1)
                n = 128 if t < T - 1 else LAST
                g = gate[0:n, t, e:e + 1] if isinstance(e, int) else gate[0:n, t, bass.ds(e, 1)]
                total, total_low = res[0:n, t, :], res_low[0:n, t, :]
                nc.vector.scalar_tensor_tensor(out=total, in0=tokP[0:n, bank, 0:D], scalar=g, in1=total, op0=ALU.mult, op1=ALU.add)
                if first:
                    last = nc.vector.tensor_scalar(total_low, tokP[0:n, bank, D:2 * D], g, None, ALU.mult)
                else:
                    last = nc.vector.scalar_tensor_tensor(out=total_low, in0=tokP[0:n, bank, D:2 * D], scalar=g, in1=total_low,
                                                          op0=ALU.mult, op1=ALU.add)
                last.then_inc(summed, 1)

            def stage(e, u, first=False):
                for j in range(FC):
                    low(e + 2, u, j)
                    hidden_low(e + 1, 1 - u, j)
                    if j >= 1:
                        if j == 1 and not first:
                            dve.wait_ge(summed, e * T)
                        add_expert(e, u, j - 1, first)

            stage(0, 0, True)
            with dve.Fori(1, E // 2) as i:
                stage(i * 2 - 1, 1)
                stage(i * 2, 0)
            dve.wait_ge(summed, (E - 1) * T)
            for t in range(T):
                add_expert(E - 1, 1, t)
                dve.wait_ge(summed, (E - 1) * T + t + 1)
                n = 128 if t < T - 1 else LAST
                nc.vector.tensor_tensor(res[0:n, t, :], res[0:n, t, :], res_low[0:n, t, :], ALU.add).then_inc(res_ready, 1)


def kernel(x, L0_tok_proj_w, L0_tok_proj_b, L0_tok_cls_token, L0_tok_pos_embedding, L0_attn_W_qkv, L0_attn_W_proj,
           L0_attn_b_proj, L0_attn_gamma, L0_attn_beta, L0_attn_random_features, L0_ffn_router_w, L0_ffn_w1, L0_ffn_w2):
    import concourse.bacc as bacc
    from concourse.bass_utils import run_bass_kernel_spmd

    f32 = np.float32

    def rows(a, n):
        return np.concatenate([a, np.zeros((n - a.shape[0], a.shape[1]), f32)])

    hp = IMG // PATCH
    patches = np.asarray(x).reshape(B, C, hp, PATCH, hp, PATCH).transpose(1, 3, 5, 0, 2, 4).reshape(KC * 128, B, NP)
    xT = np.zeros((KC * 128, TP), f32)
    xT[:, :TOK].reshape(KC * 128, B, N)[:, :, 1:] = patches
    xT = xT.reshape(KC, 128, T, 128).transpose(2, 1, 0, 3).reshape(T, 128, KC * 128)
    embed_w = np.asarray(L0_tok_proj_w).T.reshape(KC, 128, D).transpose(1, 0, 2).reshape(128, KC * D)
    token = np.arange(TP)
    pick = np.zeros((N + 2, TP), f32)
    pick[token[:TOK] % N, token[:TOK]] = 1
    pick[N, :TOK] = token[:TOK] % N == 0
    pick[N + 1, :TOK] = token[:TOK] % N != 0
    pos_w = np.concatenate([np.concatenate([np.asarray(L0_tok_pos_embedding)[0], np.asarray(L0_tok_cls_token)[0],
                                            np.asarray(L0_tok_proj_b)[None]]), pick], axis=1)
    w = np.asarray(L0_attn_W_qkv)
    g = HG * DH
    w_qk = np.concatenate([w[:, D * part + g * i:D * part + g * (i + 1)] for i in range(NG) for part in (0, 1)], axis=1)
    w_v = w[:, 2 * D:]
    rf = np.zeros((128, HG * M), f32)
    for i in range(HG):
        rf[DH * i:DH * (i + 1), M * i:M * (i + 1)] = np.asarray(L0_attn_random_features).T
        rf[64 + DH * i:64 + DH * (i + 1), M * i:M * (i + 1)] = -0.5
    image = np.zeros((128, 4), f32)
    image[np.arange(IT * N), np.arange(IT * N) // N] = 1
    w_p = np.asarray(L0_attn_W_proj)
    w_r = np.asarray(L0_ffn_router_w).T
    wide = [np.broadcast_to(np.asarray(a).reshape(1, -1), (128, a.size))
            for a in (L0_attn_gamma, L0_attn_beta, np.tril(np.ones((E, E), f32), -1))]
    att_a = np.concatenate([w_qk[:128], w_v[:128], rf, image], axis=1)
    att_b = np.concatenate([w_p[:128], w_r[:128], *wide], axis=1)
    att_r = np.concatenate([rows(w_qk[128:], DR + 1), rows(w_v[128:], DR + 1),
                            np.concatenate([w_p[128:], np.asarray(L0_attn_b_proj)[None]]), rows(w_r[128:], DR + 1)], axis=1)
    w1 = np.asarray(L0_ffn_w1).reshape(E, D, FC, 128)
    w2 = np.asarray(L0_ffn_w2).reshape(E, FC, 128, D).transpose(0, 2, 1, 3)
    expert_w = np.zeros((E + 1, 128, FC, WB), f32)
    expert_w[:E, :, :, 0:128] = w1[:, :128]
    expert_w[:E, :DR, :, 128:256] = w1[:, 128:]
    expert_w[:E, DR:, :, 128:256] = w1[:, 128:]
    expert_w[1:, :, :, 256:] = w2
    expert_w = expert_w.reshape(E + 1, 128, FC * WB)

    nc = bacc.Bacc("TRN2", target_bir_lowering=False, num_devices=1)
    arrays, args = {}, []
    for name, a in (("xT", xT), ("embed_w", embed_w), ("pos_w", pos_w), ("ident_w", np.eye(128, dtype=f32)), ("att_a", att_a),
                    ("att_b", att_b), ("att_r", att_r), ("expert_w", expert_w)):
        arrays[name] = np.ascontiguousarray(a)
        args.append(nc.dram_tensor(name, a.shape, F32, kind="ExternalInput").ap())
    args.append(nc.dram_tensor("out", (TOK, D), F32, kind="ExternalOutput").ap())
    vit_tower(nc, *args)
    r = run_bass_kernel_spmd(nc, [arrays], core_ids=[0])
    return r.results[0]["out"].reshape(B, N, D)
```

```python
from contextlib import ExitStack

import numpy as np

import concourse.bass as bass
from concourse import mybir
from concourse.alu_op_type import AluOpType as ALU

ACT = mybir.ActivationFunctionType
AX = mybir.AxisListType
F32 = mybir.dt.float32
F32R = mybir.dt.float32r

B, C, IMG, PATCH = 16, 3, 96, 16
NP = (IMG // PATCH) ** 2
N = NP + 1
TOK = B * N
HALF = TOK // 2
D = 192
DR = D - 128
KC = PATCH * PATCH * C // 128
T = -(-TOK // 128)
TP = 128 * T
LAST = TOK - 128 * (T - 1)
H, DH, M = 12, 16, 64
PAIRS = H // 2
HG = 4
NG = H // HG
IT = 3
S = -(-B // IT)
LATE = 2 * IT * N
VW = DH + 1
E, F = 8, 768
FC = F // 128
WB = 2 * 128 + D
LN_EPS = 1e-5
DEN_EPS = 1e-6

QKV = NG * 128 + D
A_QK, A_V, A_RF, A_MASK = 0, NG * 128, QKV, QKV + HG * M
A_END = A_MASK + 4
B_P, B_R, B_GAM, B_BET, B_TRI = 0, D, D + E, 2 * D + E, 3 * D + E
B_END = B_TRI + E * E
R_QK, R_V, R_P, R_R = 0, NG * 128, NG * 128 + D, NG * 128 + 2 * D
R_END = R_R + E


def vit_tower(nc, xT, embed_w, pos_w, ident_w, att_a, att_b, att_r, expert_w, out):
    ctx = ExitStack()
    with ctx:
        def sb(name, shape, dt=F32):
            return ctx.enter_context(nc.sbuf_tensor(name, shape, dt))

        def psum(name, shape):
            return ctx.enter_context(nc.psum_tensor(name, shape, F32))

        def sem(name):
            return ctx.enter_context(nc.semaphore(name))

        tokP = psum("tokP", [128, 2, 512])
        turnP = psum("turnP", [128, 2, 512])
        featP = psum("featP", [128, 2, 2, 512])

        ident = sb("ident", [128, 128])
        wa = sb("wa", [128, A_END])
        wb = sb("wb", [128, B_END])
        wr = sb("wr", [DR + 1, R_END])

        h = sb("h", [128, T, D])
        spare = sb("spare", [128, 128])
        hb = sb("hb", [128, T, D])
        xn1 = sb("xn1", [128, T, D])
        nmr = sb("nmr", [128, T])
        stat = sb("stat", [128, 3, T, 6])
        mv = sb("mv", [128, 3, T, 2])
        ve = sb("ve", [128, 3, T])
        rstd = sb("rstd", [128, 3, T])
        mhalf = sb("mhalf", [128, 1])
        table_probe = sb("table_probe", [128, 1])
        den = sb("den", [128, 4, 2 * H])
        rden = sb("rden", [128, 4, 2 * H])
        oTa = sb("oTa", [128, TP])
        oTb = sb("oTb", [DR + 1, TP])
        res = sb("res", [128, T, D])
        xn2 = sb("xn2", [128, T, 256])
        lmax = sb("lmax", [128, T])
        lg = sb("lg", [128, T, E])
        pe_ = sb("pexp", [128, T, E])
        psumr = sb("psumr", [128, T])
        prec = sb("prec", [128, T])
        prob = sb("prob", [128, T, E])
        beats = sb("beats", [128, T, E, E])
        ties = sb("ties", [128, T, E, E])
        rank = sb("rank", [128, T, E])
        gate = sb("gate", [128, T, E])
        x2 = sb("x2", [128, 2, TP])
        xh = sb("xh", [128, 2, TP], F32R)
        xl = sb("xl", [128, TP], F32R)
        w_raw = sb("w_raw", [128, 2, FC, WB])
        whl = sb("whl", [128, 2, FC, 2, WB], F32R)
        wh, wl = whl[:, :, :, 0, :], whl[:, :, :, 1, :]

        attention = ExitStack()

        def early_sb(name, shape, dt=F32):
            return attention.enter_context(nc.sbuf_tensor(name, shape, dt))

        with ExitStack() as embedding:
            x_sb = embedding.enter_context(nc.sbuf_tensor("x_sb", [128, T, KC * 128], F32))
            embed_sb = embedding.enter_context(nc.sbuf_tensor("embed_sb", [128, KC, D], F32))
            pos_sb = embedding.enter_context(nc.sbuf_tensor("pos_sb", [N + 2, D + TP], F32))
        qp = early_sb("qp", [128, PAIRS, TOK])
        qa = early_sb("qa", [128, NG, TOK])
        ka = early_sb("ka", [128, NG, TOK])
        kp = early_sb("kp", [IT * N, 2, H * M])
        vm = early_sb("vm", [IT * N, 2, IT, H, VW])
        kv = early_sb("kv", [128, B, PAIRS, 2 * VW])
        o = early_sb("o", [128, 4, 2 * H, DH])
        w_in_h = early_sb("w_in_h", [128, 2, QKV + HG * M], F32R)
        w_in_l = early_sb("w_in_l", [128, 2, QKV + HG * M], F32R)
        qh = early_sb("qh", [128, NG - 1, TOK], F32R)
        ql = early_sb("ql", [128, NG - 1, TOK], F32R)
        kh = early_sb("kh", [128, NG, TOK - LATE], F32R)
        kl = early_sb("kl", [128, NG, TOK - LATE], F32R)
        attention.close()
        act_full = sb("act_full", [128, 2, TOK])
        res_low = sb("res_low", [128, T, D])
        hh = sb("hh", [128, 2, FC, TOK], F32R)
        hl = sb("hl", [128, 2, FC, TOK], F32R)

        x_landed = [sem(f"x_landed{t}") for t in range(T)]
        embed_landed = [sem(f"embed_landed{n}") for n in range(2)]
        first_landed = [sem(f"first_landed{n}") for n in range(2)]
        pos_landed = sem("pos_landed")
        ident_landed = sem("ident_landed")
        wa_landed = sem("wa_landed")
        wb_landed = sem("wb_landed")
        wr_landed = sem("wr_landed")
        w_landed = [sem(f"w_landed{u}") for u in range(2)]
        w_high = sem("w_high")
        w_split = sem("w_split")
        x2_high = sem("x2_high")
        x2_split = sem("x2_split")
        hid_split = sem("hid_split")
        out_stored = sem("out_stored")
        pool_const = sem("pool_const")
        spare_ready = sem("spare_ready")
        embed_done = sem("embed_done")
        h_ready = sem("h_ready")
        ve_ready = [sem(f"ve_ready{n}") for n in range(3)]
        rstd_ready = [sem(f"rstd_ready{n}") for n in range(3)]
        hb_ready = sem("hb_ready")
        xn_ready = sem("xn_ready")
        turned = sem("turned")
        win_high = sem("win_high")
        win_split = sem("win_split")
        xT_high = sem("xT_high")
        xT_split = sem("xT_split")
        x2_ready = sem("x2_ready")
        qk_done = sem("qk_done")
        q_copied = sem("q_copied")
        q_first = sem("q_first")
        proj_high = sem("proj_high")
        proj_split = sem("proj_split")
        q_ready = sem("q_ready")
        k_ready = sem("k_ready")
        v_done = sem("v_done")
        vm_ready = sem("vm_ready")
        kproj_done = sem("kproj_done")
        qproj_done = sem("qproj_done")
        kp_ready = sem("kp_ready")
        qp_ready = sem("qp_ready")
        kv_done = sem("kv_done")
        kv_low = sem("kv_low")
        kv_high = sem("kv_high")
        att_done = sem("att_done")
        bank_cleared = sem("bank_cleared")
        nmr_ready = sem("nmr_ready")
        xn2_ready = sem("xn2_ready")
        y_done = sem("y_done")
        o_ready = sem("o_ready")
        o_turned = sem("o_turned")
        oT_ready = sem("oT_ready")
        router_done = sem("router_done")
        lg_ready = sem("lg_ready")
        pexp_ready = sem("pexp_ready")
        up_done = sem("up_done")
        hid_ready = sem("hid_ready")
        down_done = sem("down_done")
        summed = sem("summed")
        res_ready = sem("res_ready")
        dve_step = sem("dve_step")

        def y_tile(t):
            return featP[:, 1 - t // 2, t % 2, 0:D] if t < 4 else tokP[:, 1, 0:D]

        k_splits = [(ka[:, g, LATE:], kh[:, g], kl[:, g]) for g in range(NG)]
        q_splits = [(qa[:, g + 1], qh[:, g], ql[:, g]) for g in range(NG - 1)]
        SPLITS = [q_splits[0], *k_splits, q_splits[1]]
        HIGH_AFTER = [(1, 2, 3), (4,)]
        LOW_AFTER = [(0,), (1, 2, 3), (4,)]

        block = ctx.enter_context(nc.Block())

        @block.sync
        def _(sp):
            for half in range(2):
                c, w = KC * 128 // 2, KC * D // 2
                sp.dma_start(embed_sb[:].rearrange("p c d -> p (c d)")[:, w * half:w * (half + 1)],
                             embed_w[:, w * half:w * (half + 1)]).then_inc(embed_landed[half], 16)
                sp.dma_start(x_sb[:, 0, c * half:c * (half + 1)], xT[0][:, c * half:c * (half + 1)]).then_inc(first_landed[half], 16)
            sp.dma_start(pos_sb[:], pos_w).then_inc(pos_landed, 16)
            sp.dma_start(x_sb[:, 1, :], xT[1]).then_inc(x_landed[1], 16)
            sp.dma_start(wr[:], att_r).then_inc(wr_landed, 16)
            sp.dma_start(wa[:], att_a).then_inc(wa_landed, 16)
            sp.dma_start(ident[:], ident_w).then_inc(ident_landed, 16)
            sp.dma_start(x_sb[:, 2, :], xT[2]).then_inc(x_landed[2], 16)
            sp.dma_start(x_sb[:, 3, :], xT[3]).then_inc(x_landed[3], 16)
            sp.dma_start(x_sb[:, 4, :], xT[4]).then_inc(x_landed[4], 16)
            sp.dma_start(wb[:], att_b).then_inc(wb_landed, 16)
            for k in range(2):
                sp.dma_start(w_raw[:, k].rearrange("p c w -> p (c w)"), expert_w[k]).then_inc(w_landed[k], 16)

            def load(k, u):
                sp.wait_ge(w_split, (k - 1) * FC)
                src = expert_w[k] if isinstance(k, int) else expert_w[bass.ds(k, 1)].rearrange("k p w -> (k p) w")
                sp.dma_start(w_raw[:, u].rearrange("p c w -> p (c w)"), src).then_inc(w_landed[u], 16)

            sp.wait_ge(w_split, 2 * FC)
            with sp.Fori(1, E // 2) as i:
                load(i * 2, 0)
                load(i * 2 + 1, 1)
            load(E, 0)
            for t in range(T):
                n = 128 if t < T - 1 else LAST
                sp.wait_ge(res_ready, t + 1)
                sp.dma_start(out[128 * t:128 * t + n, :], res[0:n, t, :]).then_inc(out_stored, 16)
            sp.wait_ge(out_stored, 16 * T)

        @block.gpsimd
        def _(pool):
            nc.gpsimd.memset(mhalf[:], -0.5).then_inc(pool_const, 1)
            nc.gpsimd.memset(kv[:], 0.0).then_inc(pool_const, 1)
            nc.gpsimd.memset(oTa[:, TOK:TP], 0.0).then_inc(pool_const, 1)
            nc.gpsimd.memset(oTb[0:DR, TOK:TP], 0.0).then_inc(pool_const, 1)
            pool.wait_ge(pool_const, 4)
            nc.gpsimd.memset(oTb[DR:DR + 1, :], 1.0).then_inc(pool_const, 1)
            pool.wait_ge(pool_const, 5)

            def inverse_root(norm, t):
                pool.wait_ge(ve_ready[norm], t + 1)
                nc.gpsimd.tensor_tensor(rstd[:, norm, t:t + 1], ve[:, norm, t:t + 1], mhalf[:], ALU.pow).then_inc(rstd_ready[norm], 1)

            for t in range(T):
                inverse_root(0, t)
            for i in (1, 2, 4, 5):
                n, g = i // NG, i % NG
                c = slice(HALF * n, HALF * (n + 1))
                pool.wait_ge(q_copied, i + 1)
                nc.gpsimd.tensor_tensor(qa[64:128, g, c], qa[0:64, g, c], qa[0:64, g, c], ALU.mult).then_inc(q_ready, 1)
            pool.wait_ge(q_ready, 2 * NG - 2)
            pool.wait_ge(wb_landed, 16)
            for t in range(T):
                nc.gpsimd.tensor_tensor(hb[:, t, :], h[:, t, :], wb[:, B_BET:B_BET + D], ALU.add).then_inc(hb_ready, 1)
            for t in range(T + 1):
                if t < T:
                    inverse_root(1, t)
                if t >= 1:
                    inverse_root(2, t - 1)

        @block.scalar
        def _(act):
            act.wait_ge(wr_landed, 16)
            for at in (0, DR):
                nc.scalar.copy(w_in_h[at:at + DR, 1, 0:QKV], wr[0:DR, R_QK:R_QK + QKV]).then_inc(win_high, 1)

            def x_high(t):
                act.wait_ge(turned, t + 1)
                c = slice(128 * t, 128 * (t + 1))
                nc.scalar.copy(xh[:, 0, c], turnP[:, t % 2, 0:128]).then_inc(xT_high, 1)
                nc.scalar.copy(xh[0:DR, 1, c], turnP[0:DR, t % 2, 128:256]).then_inc(xT_high, 1)

            for t in range(T):
                act.wait_ge(embed_done, t + 1)
                nc.scalar.copy(h[:, t, :], tokP[:, t % 2, 0:D]).then_inc(h_ready, 1)
                if t == 0:
                    act.wait_ge(wa_landed, 16)
                    nc.scalar.copy(w_in_h[:, 0, :], wa[:, A_QK:A_MASK]).then_inc(win_high, 1)
                if t >= 1:
                    x_high(t - 1)
            for i in range(2 * NG):
                if i == 1:
                    x_high(T - 1)
                n, g = i // NG, i % NG
                c = slice(HALF * n, HALF * (n + 1))
                act.wait_ge(qk_done, i + 1)
                nc.scalar.copy(ka[0:64, g, c], featP[64:128, (i // 2) % 2, i % 2, 0:HALF])
                nc.scalar.activation(ka[64:128, g, c], featP[64:128, (i // 2) % 2, i % 2, 0:HALF], ACT.Square).then_inc(k_ready, 1)

            def kv_rows_high(s):
                n = min(IT, B - IT * s)
                act.wait_ge(kv_done, s + 1)
                nc.scalar.activation(
                    kv[64:128, IT * s:IT * s + n, :, VW:2 * VW].rearrange("p i h v -> p h i v"),
                    turnP[64:128].rearrange("p b (h c) -> p (b h) c", c=128)[:, 0:PAIRS, 0:2 * VW * n].rearrange("p h (i v) -> p h i v", i=n)[:, :, :, VW:2 * VW],
                    ACT.Copy, scale=1.0 / M).then_inc(kv_high, 1)

            def high(k, u, j, cols=slice(0, WB)):
                nc.scalar.copy(wh[:, u, j, cols], w_raw[:, u, j, cols]).then_inc(w_high, 1)

            def proj_high_part(i):
                full, high_part, _ = SPLITS[i]
                if i in (0, 4):
                    act.wait_ge(q_copied, NG + (2 if i == 0 else 3))
                    act.wait_ge(q_ready, 3 if i == 0 else 4)
                else:
                    act.wait_ge(k_ready, 2 * NG)
                nc.scalar.copy(high_part, full).then_inc(proj_high, 1)

            def query_exp(s):
                act.wait_ge(qproj_done, s + 1)
                nc.scalar.activation(qp[:, s, :].rearrange("p (n t) -> p n t", n=2), featP[:, 1, :, 0:HALF], ACT.Exp).then_inc(qp_ready, 1)

            act.wait_ge(pool_const, 5)
            act.wait_ge(w_landed[0], 16)
            act.wait_ge(w_landed[1], 16)
            query_exp(0)
            proj_high_part(0)
            for s in range(S):
                rows = min(IT, B - IT * s) * N
                act.wait_ge(kproj_done, s + 1)
                if s >= 2:
                    act.wait_ge(kv_done, s - 1)
                nc.scalar.activation(kp[0:rows, s % 2, :], featP[0:rows, 0].rearrange("p b c -> p (b c)")[:, 0:H * M], ACT.Exp).then_inc(kp_ready, 1)
                if s + 1 < PAIRS:
                    query_exp(s + 1)
                if s < len(HIGH_AFTER):
                    for i in HIGH_AFTER[s]:
                        proj_high_part(i)
                if s >= 1:
                    kv_rows_high(s - 1)
                high(0, 0, s, slice(0, 256))
                high(1, 1, s)
            kv_rows_high(S - 1)

            def take_oT(k):
                act.wait_ge(o_turned, k + 1)
                c = slice(4 * N * k, 4 * N * (k + 1))
                for dst, at, rows in ((oTa, 0, 128), (oTb, 256, DR)):
                    nc.scalar.copy(dst[0:rows, c].rearrange("p (i n) -> p i n", n=N),
                                   turnP[0:rows, k % 2, at:at + 256].rearrange("p (i n) -> p i n", n=64)[:, :, 0:N]).then_inc(oT_ready, 1)

            for k in range(4):
                take_oT(k)

            nc.scalar.activation(table_probe[:], mhalf[:], ACT.Gelu_apprx_tanh)
            for t in range(T + 1):
                if t < T:
                    act.wait_ge(nmr_ready, t + 1)
                    nc.scalar.activation(xn2[:, t, 0:D], res[:, t, :], ACT.Identity, bias=nmr[:, t:t + 1],
                                         scale=rstd[:, 2, t:t + 1]).then_inc(xn2_ready, 1)
                    nc.scalar.activation(xn2[:, t, D:256], res[:, t, 128:D], ACT.Identity, bias=nmr[:, t:t + 1],
                                         scale=rstd[:, 2, t:t + 1]).then_inc(xn2_ready, 1)
                if t >= 1:
                    act.wait_ge(turned, T + t)
                    c = slice(128 * (t - 1), 128 * t)
                    src = turnP[:, (t - 1) % 2, 0:256].rearrange("p (h n) -> p h n", h=2)
                    nc.scalar.copy(xh[:, :, c], src).then_inc(x2_high, 1)
                    nc.scalar.copy(x2[:, :, c], src).then_inc(x2_ready, 1)

            def gelu(e, u, j, first=False):
                act.wait_ge(up_done, e * FC + j + 1)
                src = featP[:, j % 2, :, 0:HALF]
                nc.scalar.activation(hh[:, u, j, 0:TOK].rearrange("p (n t) -> p n t", n=2), src, ACT.Gelu_apprx_tanh)
                if not (first and j < 2):
                    act.wait_ge(hid_split, e * FC + j - 1)
                nc.scalar.activation(act_full[:, j % 2, :].rearrange("p (n t) -> p n t", n=2), src,
                                     ACT.Gelu_apprx_tanh).then_inc(hid_ready, 1)

            def stage(e, u, first=False):
                act.wait_ge(w_landed[u], (e - u) * 8 + 32)
                act.wait_ge(up_done if first else down_done, FC if first else e * T)
                for j in range(FC):
                    high(e + 2, u, j)
                    gelu(e + 1, 1 - u, j)
                    if first and j == 0:
                        act.wait_ge(lg_ready, 1)
                        nc.scalar.activation(pe_[:], lg[:], ACT.Exp).then_inc(pexp_ready, 1)

            for j in range(FC):
                gelu(0, 0, j, True)
            stage(0, 0, True)
            with act.Fori(1, E // 2) as i:
                stage(i * 2 - 1, 1)
                stage(i * 2, 0)

        @block.tensor
        def _(pe):
            def keep_clock(n, bank=0):
                for _ in range(n):
                    pe.matmul(tokP[:, bank, 256:384], spare[:], spare[:], start=True, stop=True)

            def turn(t):
                pe.wait_ge(xn_ready, t + 1)
                if t >= 2:
                    pe.wait_ge(xT_split, 2 * (t - 1))
                pe.transpose(turnP[:, t % 2, 0:128], xn1[:, t, 0:128], ident[:])
                pe.transpose(turnP[0:DR, t % 2, 128:256], xn1[:, t, 128:D], ident[:]).then_inc(turned, 1)

            pe.wait_ge(spare_ready, 1)
            keep_clock(8)
            for t in range(T):
                if t > 0:
                    pe.wait_ge(x_landed[t], 16)
                if t >= 2:
                    pe.wait_ge(h_ready, t - 1)
                for c in range(KC):
                    if t == 0 and c % (KC // 2) == 0:
                        pe.wait_ge(embed_landed[c // (KC // 2)], 16)
                        pe.wait_ge(first_landed[c // (KC // 2)], 16)
                    pe.matmul(tokP[:, t % 2, 0:D], x_sb[:, t, 128 * c:128 * (c + 1)], embed_sb[:, c, :], start=(c == 0), stop=False)
                if t == 0:
                    pe.wait_ge(pos_landed, 16)
                pe.matmul(tokP[:, t % 2, 0:D], pos_sb[:, D + 128 * t:D + 128 * (t + 1)], pos_sb[:, 0:D], start=False, stop=True).then_inc(embed_done, 1)
                if t == 2:
                    pe.wait_ge(ident_landed, 16)
                if t >= 2:
                    turn(t - 2)

            def values(s):
                rows = min(IT, B - IT * s) * N
                c = slice(IT * N * s, IT * N * s + rows)
                v = slice(NG * 128, QKV)
                if s >= 2:
                    pe.wait_ge(vm_ready, s - 1)
                terms = [(xh[:, 0, c], w_in_h[:, 0, v]), (xh[:, 0, c], w_in_l[:, 0, v]), (xl[:, c], w_in_h[:, 0, v]),
                         (xh[:, 1, c], w_in_h[:, 1, v]),
                         (xh[0:DR, 1, c], w_in_l[0:DR, 1, v])]
                for k, (x, weights) in enumerate(terms):
                    mm = pe.matmul(tokP[0:rows, s % 2, 0:D], x, weights, start=(k == 0), stop=(k == len(terms) - 1))
                mm.then_inc(v_done, 1)

            turn(T - 2)
            pe.wait_ge(win_split, 2)
            pe.wait_ge(win_high, 3)
            pe.wait_ge(xT_split, 4)
            pe.wait_ge(h_ready, T - 1)
            values(1)

            for i in range(2 * NG):
                n, g = i // NG, i % NG
                if i == 2:
                    turn(T - 1)
                if i == NG:
                    pe.wait_ge(h_ready, T)
                    values(0)
                pe.wait_ge(xT_split, 2 * (3 if n == 0 else T))
                if i >= 4:
                    pe.wait_ge(q_copied, i - 3)
                    pe.wait_ge(k_ready, i - 3)
                c = slice(HALF * n, HALF * (n + 1))
                bank = featP[:, (i // 2) % 2, i % 2, 0:HALF]
                w = slice(128 * g, 128 * (g + 1))
                terms = [(w_in_h[:, 0, w], xh[:, 0, c]), (w_in_h[:, 0, w], xl[:, c]), (w_in_l[:, 0, w], xh[:, 0, c]),
                         (w_in_h[:, 1, w], xh[:, 1, c]), (w_in_l[0:DR, 1, w], xh[0:DR, 1, c])]
                for k, (weights, x) in enumerate(terms):
                    mm = pe.matmul(bank, weights, x, start=(k == 0), stop=(k == len(terms) - 1))
                mm.then_inc(qk_done, 1)

            def key_sums(s):
                n = min(IT, B - IT * s)
                pe.wait_ge(kp_ready, s + 1)
                pe.wait_ge(vm_ready, s + 1)
                if s >= 1:
                    pe.wait_ge(kv_low, s)
                    pe.wait_ge(kv_high, s)
                for p in range(PAIRS):
                    mm = pe.matmul(turnP[:, p // 4, 128 * (p % 4):128 * (p % 4) + 2 * VW * n].rearrange("p (i v) -> p i v", i=n),
                                   kp[0:n * N, s % 2, 128 * p:128 * (p + 1)],
                                   vm[0:n * N, s % 2, 0:n, 2 * p:2 * p + 2, :].rearrange("p i h v -> p i (h v)"), start=True, stop=True)
                mm.then_inc(kv_done, 1)

            rf_h, rf_l = w_in_h[:, 0, QKV:], w_in_l[:, 0, QKV:]

            def query_features(s):
                g = s // 2
                if g == 0:
                    pe.wait_ge(q_first, 2)
                else:
                    pe.wait_ge(q_ready, g + 2)
                if s == 0:
                    pe.wait_ge(k_ready, 4)
                else:
                    pe.wait_ge(qp_ready, s)
                w = slice(128 * (s % 2), 128 * (s % 2 + 1))
                if g == 0:
                    terms = [(wa[:, A_RF:A_MASK][:, w], qa[:, 0])]
                else:
                    pe.wait_ge(proj_split, 1 if g == 1 else 5)
                    terms = [(rf_h[:, w], qh[:, g - 1]), (rf_h[:, w], ql[:, g - 1]), (rf_l[:, w], qh[:, g - 1])]
                for k, (weights, q) in enumerate(terms):
                    for n in range(2):
                        mm = pe.matmul(featP[:, 1, n, 0:HALF], weights, q[:, HALF * n:HALF * (n + 1)],
                                       start=(k == 0), stop=(k == len(terms) - 1))
                mm.then_inc(qproj_done, 1)

            query_features(0)
            for s in range(S):
                rows = min(IT, B - IT * s) * N
                c = slice(IT * N * s, IT * N * s + rows)
                if s == 0:
                    pe.wait_ge(k_ready, 2 * NG)
                    pe.wait_ge(q_copied, 2 * NG)
                else:
                    pe.wait_ge(kp_ready, s)
                if s < 2:
                    terms = [(ka, wa[:, A_RF:A_MASK])]
                else:
                    pe.wait_ge(proj_split, 4)
                    terms = [(kh, rf_h), (kl, rf_h), (kh, rf_l)]
                    c = slice(c.start - LATE, c.stop - LATE)
                for g in range(NG):
                    for k, (keys, weights) in enumerate(terms):
                        mm = pe.matmul(featP[0:rows, 0, g // 2, 256 * (g % 2):256 * (g % 2) + HG * M], keys[:, g, c], weights,
                                       start=(k == 0), stop=(k == len(terms) - 1))
                mm.then_inc(kproj_done, 1)
                if s + 1 < PAIRS:
                    query_features(s + 1)
                if s >= 1:
                    key_sums(s - 1)
                if s + 2 < S:
                    values(s + 2)

            def router(t):
                pe.wait_ge(x2_ready, t + 1)
                c = slice(128 * t, 128 * (t + 1))
                logits = tokP[:, 0, E * t:E * (t + 1)]
                pe.matmul(logits, x2[:, 0, c], wb[:, B_R:B_R + E], start=True, stop=False)
                pe.matmul(logits, x2[0:DR, 1, c], wr[0:DR, R_R:R_R + E], start=False, stop=True).then_inc(router_done, 1)

            def project(t):
                if t == 0:
                    pe.wait_ge(wb_landed, 16)
                if t == T - 1:
                    pe.wait_ge(vm_ready, S)
                pe.wait_ge(oT_ready, 2 * (-(-min(128 * (t + 1), TOK) // (4 * N))))
                c = slice(128 * t, 128 * (t + 1))
                y = y_tile(t)
                pe.matmul(y, ident[:], xn1[:, t, :], start=True, stop=False)
                pe.matmul(y, oTa[:, c], wb[:, B_P:B_P + D], start=False, stop=False)
                pe.matmul(y, oTb[:, c], wr[:, R_P:R_P + D], start=False, stop=True).then_inc(y_done, 1)

            def turn_o(k):
                if k == 0:
                    pe.wait_ge(kv_low, S)
                    pe.wait_ge(kv_high, S)
                pe.wait_ge(o_ready, k + 1)
                if k >= 2:
                    pe.wait_ge(oT_ready, 2 * (k - 1))
                for gg in range(2):
                    f = o[:, k, H * gg:H * (gg + 1), :].rearrange("p h d -> p (h d)")
                    pe.transpose(turnP[:, k % 2, 128 * gg:128 * (gg + 1)], f[:, 0:128], ident[:])
                    mm = pe.transpose(turnP[0:DR, k % 2, 256 + 128 * gg:256 + 128 * (gg + 1)], f[:, 128:D], ident[:])
                mm.then_inc(o_turned, 1)

            pe.wait_ge(qp_ready, PAIRS)
            pe.wait_ge(bank_cleared, 1)
            for k in range(4):
                tiles = -(-min(4 * (k + 1), B) // IT)
                pe.wait_ge(kv_low, tiles)
                pe.wait_ge(kv_high, tiles)
                for gg in range(2):
                    for half in range(2):
                        b = 4 * k + 2 * gg + half
                        for p in range(PAIRS):
                            at = 2 * VW * (PAIRS * gg + p)
                            mm = pe.matmul(featP[64 * half:64 * half + N, 1 - k // 2, k % 2, at:at + 2 * VW],
                                           qp[:, p, N * b:N * (b + 1)], kv[:, b, p, :], start=True, stop=True)
                mm.then_inc(att_done, 1)
                if k == 0:
                    key_sums(S - 1)
                if k >= 1:
                    turn_o(k - 1)
                if k >= 2:
                    project(k - 2)
            turn_o(3)
            for t in range(2, T):
                project(t)

            def up(e, u, j, first=False, halves=(0, 1)):
                pe.wait_ge(w_split, 2 * j + 1 if first else e * FC + j + 1)
                if not (first and j < 2):
                    pe.wait_ge(hid_ready, e * FC + j - 1)
                a, b = slice(0, 128), slice(128, 256)
                terms = [(wh[:, u, j, a], xh[:, 0]), (wh[:, u, j, a], xl[:]), (wl[:, u, j, a], xh[:, 0]),
                         (wh[:, u, j, b], xh[:, 1]),
                         (wl[0:DR, u, j, b], xh[0:DR, 1])]
                for k, (weights, x) in enumerate(terms):
                    for n in halves:
                        mm = pe.matmul(featP[:, j % 2, n, 0:HALF], weights, x[:, HALF * n:HALF * (n + 1)],
                                       start=(k == 0), stop=(k == len(terms) - 1))
                if 1 in halves:
                    mm.then_inc(up_done, 1)

            def down(e, u, t, first=False):
                bank = (u * T + t) % 2
                if first and t < 2:
                    if t == 0:
                        pe.wait_ge(lg_ready, 1)
                elif isinstance(e, int) and e == E - 1 and t >= 2:
                    pe.wait_ge(res_ready, t - 1)
                else:
                    pe.wait_ge(summed, e * T + t - 1)
                n = 128 if t < T - 1 else LAST
                c = slice(128 * t, 128 * t + n)
                w = slice(256, WB)
                for j in range(FC):
                    if t == 0:
                        pe.wait_ge(w_split, e * FC + FC + j + 1)
                        pe.wait_ge(hid_split, e * FC + j + 1)
                    pe.matmul(tokP[0:n, bank, 0:2 * D].rearrange("p (k d) -> p k d", k=2), hh[:, u, j, c], whl[:, 1 - u, j, :, w],
                              start=(j == 0), stop=(j == FC - 1), skip_group_check=True)
                    mm = pe.matmul(tokP[0:n, bank, 0:D], hl[:, u, j, c], wh[:, 1 - u, j, w], start=False, stop=(j == FC - 1), skip_group_check=True)
                mm.then_inc(down_done, 1)

            def stage(e, u, first=False):
                for j in range(FC):
                    up(e + 1, 1 - u, j)
                    if j >= 1:
                        down(e, u, j - 1, first)

            for t in range(T):
                keep_clock((8, 3, 3, 3, 2)[t])
                pe.wait_ge(xn2_ready, 2 * (t + 1))
                if t >= 2:
                    pe.wait_ge(x2_ready, t - 1)
                pe.transpose(turnP[:, t % 2, 0:128], xn2[:, t, 0:128], ident[:])
                pe.transpose(turnP[:, t % 2, 128:256], xn2[:, t, 128:256], ident[:]).then_inc(turned, 1)
                if t == T - 1:
                    pe.wait_ge(x2_split, 3)
                    up(0, 0, 0, True, (0,))
                if t >= 1:
                    router(t - 1)
            up(0, 0, 1, True, (0,))
            pe.wait_ge(x2_split, T)
            up(0, 0, 0, True, (1,))
            up(0, 0, 1, True, (1,))
            router(T - 1)
            keep_clock(3, 1)
            for j in range(2, FC):
                up(0, 0, j, True)
            stage(0, 0, True)
            with pe.Fori(1, E // 2) as i:
                stage(i * 2 - 1, 1)
                stage(i * 2, 0)
            for t in range(T):
                down(E - 1, 1, t)

        @block.vector
        def _(dve):
            steps = [0]

            def mark(ins):
                steps[0] += 1
                ins.then_inc(dve_step, 1)
                return steps[0]

            def link(ins):
                dve.wait_ge(dve_step, mark(ins))

            def moments(norm, t, src):
                link(nc.vector.bn_stats(stat[:, norm, t, :], src))
                link(nc.vector.bn_aggr(mv[:, norm, t, :], stat[:, norm, t, :]))
                add_eps(norm, t)

            def add_eps(norm, t):
                nc.vector.tensor_scalar(ve[:, norm, t:t + 1], mv[:, norm, t, 1:2], LN_EPS, None, ALU.add).then_inc(ve_ready[norm], 1)

            def normalise(norm, t, src, dst):
                dve.wait_ge(rstd_ready[norm], t + 1)
                nc.vector.tensor_scalar(dst[:, t, :], src[:, t, :], mv[:, norm, t, 0:1], rstd[:, norm, t:t + 1],
                                        ALU.subtract, ALU.mult).then_inc(xn_ready, 1)

            nc.vector.memset(spare[:], 0.0).then_inc(spare_ready, 1)
            nc.vector.memset(featP[:, :, :, HALF:2 * H * VW], 0.0).then_inc(bank_cleared, 1)
            dve.wait_ge(win_high, 1)
            nc.vector.tensor_tensor(w_in_l[0:DR, 1, 0:QKV], wr[0:DR, R_QK:R_QK + QKV], w_in_h[0:DR, 1, 0:QKV].bitcast(F32),
                                    ALU.subtract).then_inc(win_split, 1)

            def x_low(t):
                c = slice(128 * t, 128 * (t + 1))
                dve.wait_ge(xT_high, 2 * (t + 1))
                nc.vector.tensor_tensor(xl[:, c], turnP[:, t % 2, 0:128], xh[:, 0, c].bitcast(F32), ALU.subtract).then_inc(xT_split, 1)
                nc.vector.tensor_tensor(xh[DR:128, 1, c], turnP[0:DR, t % 2, 128:256], xh[0:DR, 1, c].bitcast(F32),
                                        ALU.subtract).then_inc(xT_split, 1)

            for t in range(T + 1):
                if t >= 1:
                    normalise(0, t - 1, h, xn1)
                if t >= 2:
                    x_low(t - 2)
                if t < T:
                    dve.wait_ge(h_ready, t + 1)
                    moments(0, t, h[:, t, :])
                if t == 1:
                    dve.wait_ge(win_high, 3)
                    nc.vector.tensor_tensor(w_in_l[:, 0, :], wa[:, A_QK:A_MASK], w_in_h[:, 0, :].bitcast(F32),
                                            ALU.subtract).then_inc(win_split, 1)
                if t == 4:
                    for u in range(2):
                        nc.vector.tensor_copy(vm[:, u, :, :, DH:VW].rearrange("p i h v -> p i (h v)"),
                                              wa[0:IT * N, A_MASK:A_MASK + IT].unsqueeze(2).broadcast_to([IT * N, IT, H]))

            for i in range(2 * NG):
                n, g = i // NG, i % NG
                c = slice(HALF * n, HALF * (n + 1))
                dve.wait_ge(qk_done, i + 1)
                nc.vector.tensor_copy(qa[0:64, g, c], featP[0:64, (i // 2) % 2, i % 2, 0:HALF]).then_inc(q_copied, 1)
                if i == 0:
                    x_low(T - 1)
                if g == 0:
                    dve.wait_ge(q_copied, i + 1)
                    nc.vector.tensor_tensor(qa[64:128, g, c], qa[0:64, g, c], qa[0:64, g, c], ALU.mult).then_inc(q_first, 1)

            def mask_values(s):
                n = min(IT, B - IT * s)
                rows = n * N
                dve.wait_ge(v_done, max(s + 1, 2))
                if s >= 2:
                    dve.wait_ge(kv_done, s - 1)
                nc.vector.tensor_tensor(
                    vm[0:rows, s % 2, 0:n, :, 0:DH],
                    tokP[0:rows, s % 2, 0:D].rearrange("p (h d) -> p h d", d=DH).unsqueeze(1).broadcast_to([rows, n, H, DH]),
                    wa[0:rows, A_MASK:A_MASK + n].unsqueeze(2).unsqueeze(3).broadcast_to([rows, n, H, DH]),
                    ALU.mult).then_inc(vm_ready, 1)

            def kv_rows_low(s):
                n = min(IT, B - IT * s)
                dve.wait_ge(kv_done, s + 1)
                nc.vector.tensor_scalar(
                    kv[0:64, IT * s:IT * s + n, :, 0:VW].rearrange("p i h v -> p h i v"),
                    turnP[0:64].rearrange("p b (h c) -> p (b h) c", c=128)[:, 0:PAIRS, 0:2 * VW * n].rearrange("p h (i v) -> p h i v", i=n)[:, :, :, 0:VW],
                    1.0 / M, None, ALU.mult).then_inc(kv_low, 1)

            def low(k, u, j, cols=slice(0, WB)):
                dve.wait_ge(w_high, 2 * j + k + 1 if isinstance(k, int) and k < 2 else k * FC + j + 1)
                nc.vector.tensor_tensor(wl[:, u, j, cols], w_raw[:, u, j, cols], wh[:, u, j, cols].bitcast(F32), ALU.subtract).then_inc(w_split, 1)

            dve.wait_ge(pool_const, 5)
            for s in range(S):
                mask_values(s)
                if s < len(LOW_AFTER):
                    for i in LOW_AFTER[s]:
                        full, high_part, low_part = SPLITS[i]
                        dve.wait_ge(proj_high, i + 1)
                        nc.vector.tensor_tensor(low_part, full, high_part.bitcast(F32), ALU.subtract).then_inc(proj_split, 1)
                if s >= 1:
                    kv_rows_low(s - 1)
                    low(0, 0, s - 1, slice(0, 256))
                    low(1, 1, s - 1)

            def divide(k):
                dve.wait_ge(att_done, k + 1)
                both = featP[:, 1 - k // 2, k % 2, 0:2 * H * VW].rearrange("p (h v) -> p h v", v=VW)
                link(nc.vector.tensor_scalar(den[:, k, :].unsqueeze(2), both[:, :, DH:VW], DEN_EPS, None, ALU.add))
                link(nc.vector.reciprocal(rden[:, k, :], den[:, k, :]))
                nc.vector.tensor_tensor(o[:, k], both[:, :, 0:DH], rden[:, k, :].unsqueeze(2).broadcast_to([128, 2 * H, DH]),
                                        ALU.mult).then_inc(o_ready, 1)

            divide(0)
            kv_rows_low(S - 1)
            divide(1)
            low(0, 0, S - 1, slice(0, 256))
            low(1, 1, S - 1)
            divide(2)

            dve.wait_ge(wb_landed, 16)
            dve.wait_ge(hb_ready, T)

            def x2_low(t):
                c = slice(128 * t, 128 * (t + 1))
                dve.wait_ge(x2_ready, t + 1)
                nc.vector.tensor_tensor(xl[:, c], x2[:, 0, c], xh[:, 0, c].bitcast(F32), ALU.subtract)
                nc.vector.tensor_tensor(xh[64:128, 1, c], x2[64:128, 1, c], xh[64:128, 1, c].bitcast(F32), ALU.subtract).then_inc(x2_split, 1)

            mark_of = {}

            def need(*what):
                dve.wait_ge(dve_step, mark_of[what])

            for t in range(T + 4):
                a, b, c = t, t - 1, t - 2
                if t == 1:
                    divide(3)
                if a < T:
                    dve.wait_ge(y_done, a + 1)
                    mark_of["stats1", a] = mark(nc.vector.bn_stats(stat[:, 1, a, :], y_tile(a)))
                if 0 <= b < T:
                    dve.wait_ge(rstd_ready[1], b + 1)
                    mark_of["affine", b] = mark(nc.vector.scalar_tensor_tensor(
                        out=res[:, b, :], in0=y_tile(b), scalar=mv[:, 1, b, 0:1], in1=wb[:, B_GAM:B_GAM + D], op0=ALU.subtract, op1=ALU.mult))
                if a < T:
                    need("stats1", a)
                    mark_of["mean1", a] = mark(nc.vector.bn_aggr(mv[:, 1, a, :], stat[:, 1, a, :]))
                if 0 <= b < T:
                    need("affine", b)
                    mark_of["residual", b] = mark(nc.vector.scalar_tensor_tensor(
                        out=res[:, b, :], in0=res[:, b, :], scalar=rstd[:, 1, b:b + 1], in1=hb[:, b, :], op0=ALU.mult, op1=ALU.add))
                if a < T:
                    need("mean1", a)
                    add_eps(1, a)
                if 0 <= c < T:
                    dve.wait_ge(rstd_ready[2], c + 1)
                    nc.vector.scalar_tensor_tensor(out=nmr[:, c:c + 1], in0=mv[:, 2, c, 0:1], scalar=-1.0, in1=rstd[:, 2, c:c + 1],
                                                   op0=ALU.mult, op1=ALU.mult).then_inc(nmr_ready, 1)
                if 0 <= b < T:
                    need("residual", b)
                    mark_of["stats2", b] = mark(nc.vector.bn_stats(stat[:, 2, b, :], res[:, b, :]))
                    need("stats2", b)
                    mark_of["mean2", b] = mark(nc.vector.bn_aggr(mv[:, 2, b, :], stat[:, 2, b, :]))
                    need("mean2", b)
                    add_eps(2, b)
                for d in {T: (0,), T + 1: (1, 2), T + 2: (3,), T + 3: (4,)}.get(t, ()):
                    x2_low(d)

            def hidden_low(e, u, j):
                dve.wait_ge(hid_ready, e * FC + j + 1)
                nc.vector.tensor_tensor(hl[:, u, j, 0:TOK], act_full[:, j % 2, :], hh[:, u, j, 0:TOK].bitcast(F32), ALU.subtract).then_inc(hid_split, 1)

            dve.wait_ge(router_done, T)
            logits = tokP[:, 0, 0:T * E].rearrange("p (t e) -> p t e", e=E)
            link(nc.vector.tensor_reduce(lmax[:].unsqueeze(2), logits, AX.X, ALU.max))
            nc.vector.tensor_tensor(lg[:], logits, lmax[:].unsqueeze(2).broadcast_to([128, T, E]), ALU.subtract).then_inc(lg_ready, 1)
            for j in range(FC):
                hidden_low(0, 0, j)

            def gates():
                dve.wait_ge(pexp_ready, 1)
                link(nc.vector.tensor_reduce(psumr[:].unsqueeze(2), pe_[:], AX.X, ALU.add))
                link(nc.vector.reciprocal(prec[:], psumr[:]))
                link(nc.vector.tensor_tensor(prob[:], pe_[:], prec[:].unsqueeze(2).broadcast_to([128, T, E]), ALU.mult))
                other = prob[:].unsqueeze(2).broadcast_to([128, T, E, E])
                own = prob[:].unsqueeze(3).broadcast_to([128, T, E, E])
                equal_done = mark(nc.vector.tensor_tensor(ties[:], other, own, ALU.is_equal))
                mark(nc.vector.tensor_tensor(beats[:], other, own, ALU.is_gt))
                earlier = wb[:, B_TRI:B_TRI + E * E].rearrange("p (a b) -> p a b", b=E).unsqueeze(1).broadcast_to([128, T, E, E])
                dve.wait_ge(dve_step, equal_done)
                link(nc.vector.tensor_tensor(ties[:], ties[:], earlier, ALU.mult))
                link(nc.vector.tensor_tensor(beats[:], beats[:], ties[:], ALU.add))
                link(nc.vector.tensor_reduce(rank[:].unsqueeze(3), beats[:], AX.X, ALU.add))
                link(nc.vector.scalar_tensor_tensor(out=gate[:], in0=rank[:], scalar=2.0, in1=prob[:], op0=ALU.is_lt, op1=ALU.mult))

            def add_expert(e, u, t, first=False):
                bank = (u * T + t) % 2
                dve.wait_ge(down_done, e * T + t + 1)
                n = 128 if t < T - 1 else LAST
                g = gate[0:n, t, e:e + 1] if isinstance(e, int) else gate[0:n, t, bass.ds(e, 1)]
                total, total_low = res[0:n, t, :], res_low[0:n, t, :]
                nc.vector.scalar_tensor_tensor(out=total, in0=tokP[0:n, bank, 0:D], scalar=g, in1=total, op0=ALU.mult, op1=ALU.add)
                if first:
                    last = nc.vector.tensor_scalar(total_low, tokP[0:n, bank, D:2 * D], g, None, ALU.mult)
                else:
                    last = nc.vector.scalar_tensor_tensor(out=total_low, in0=tokP[0:n, bank, D:2 * D], scalar=g, in1=total_low,
                                                          op0=ALU.mult, op1=ALU.add)
                last.then_inc(summed, 1)

            def stage(e, u, first=False):
                for j in range(FC):
                    if first and j == 1:
                        gates()
                        add_expert(0, 0, 0, True)
                    low(e + 2, u, j)
                    hidden_low(e + 1, 1 - u, j)
                    if j >= (2 if first else 1):
                        if j == 1 and not first:
                            dve.wait_ge(summed, e * T)
                        add_expert(e, u, j - 1, first)

            stage(0, 0, True)
            with dve.Fori(1, E // 2) as i:
                stage(i * 2 - 1, 1)
                stage(i * 2, 0)
            dve.wait_ge(summed, (E - 1) * T)
            for t in range(T):
                n = 128 if t < T - 1 else LAST
                g = gate[0:n, t, E - 1:E]
                total, bank = res[0:n, t, :], (T + t) % 2
                link(nc.vector.tensor_tensor(total, total, res_low[0:n, t, :], ALU.add))
                dve.wait_ge(down_done, (E - 1) * T + t + 1)
                link(nc.vector.scalar_tensor_tensor(out=total, in0=tokP[0:n, bank, D:2 * D], scalar=g, in1=total, op0=ALU.mult, op1=ALU.add))
                nc.vector.scalar_tensor_tensor(out=total, in0=tokP[0:n, bank, 0:D], scalar=g, in1=total, op0=ALU.mult,
                                               op1=ALU.add).then_inc(res_ready, 1)


def kernel(x, L0_tok_proj_w, L0_tok_proj_b, L0_tok_cls_token, L0_tok_pos_embedding, L0_attn_W_qkv, L0_attn_W_proj,
           L0_attn_b_proj, L0_attn_gamma, L0_attn_beta, L0_attn_random_features, L0_ffn_router_w, L0_ffn_w1, L0_ffn_w2):
    import concourse.bacc as bacc
    from concourse.bass_utils import run_bass_kernel_spmd

    f32 = np.float32

    def rows(a, n):
        return np.concatenate([a, np.zeros((n - a.shape[0], a.shape[1]), f32)])

    hp = IMG // PATCH
    patches = np.asarray(x).reshape(B, C, hp, PATCH, hp, PATCH).transpose(1, 3, 5, 0, 2, 4).reshape(KC * 128, B, NP)
    xT = np.zeros((KC * 128, TP), f32)
    xT[:, :TOK].reshape(KC * 128, B, N)[:, :, 1:] = patches
    xT = xT.reshape(KC, 128, T, 128).transpose(2, 1, 0, 3).reshape(T, 128, KC * 128)
    embed_w = np.asarray(L0_tok_proj_w).T.reshape(KC, 128, D).transpose(1, 0, 2).reshape(128, KC * D)
    token = np.arange(TP)
    pick = np.zeros((N + 2, TP), f32)
    pick[token[:TOK] % N, token[:TOK]] = 1
    pick[N, :TOK] = token[:TOK] % N == 0
    pick[N + 1, :TOK] = token[:TOK] % N != 0
    pos_w = np.concatenate([np.concatenate([np.asarray(L0_tok_pos_embedding)[0], np.asarray(L0_tok_cls_token)[0],
                                            np.asarray(L0_tok_proj_b)[None]]), pick], axis=1)
    w = np.asarray(L0_attn_W_qkv)
    g = HG * DH
    w_qk = np.concatenate([w[:, D * part + g * i:D * part + g * (i + 1)] for i in range(NG) for part in (0, 1)], axis=1)
    w_v = w[:, 2 * D:]
    rf = np.zeros((128, HG * M), f32)
    for i in range(HG):
        rf[DH * i:DH * (i + 1), M * i:M * (i + 1)] = np.asarray(L0_attn_random_features).T
        rf[64 + DH * i:64 + DH * (i + 1), M * i:M * (i + 1)] = -0.5
    image = np.zeros((128, 4), f32)
    image[np.arange(IT * N), np.arange(IT * N) // N] = 1
    w_p = np.asarray(L0_attn_W_proj)
    w_r = np.asarray(L0_ffn_router_w).T
    wide = [np.broadcast_to(np.asarray(a).reshape(1, -1), (128, a.size))
            for a in (L0_attn_gamma, L0_attn_beta, np.tril(np.ones((E, E), f32), -1))]
    att_a = np.concatenate([w_qk[:128], w_v[:128], rf, image], axis=1)
    att_b = np.concatenate([w_p[:128], w_r[:128], *wide], axis=1)
    att_r = np.concatenate([rows(w_qk[128:], DR + 1), rows(w_v[128:], DR + 1),
                            np.concatenate([w_p[128:], np.asarray(L0_attn_b_proj)[None]]), rows(w_r[128:], DR + 1)], axis=1)
    w1 = np.asarray(L0_ffn_w1).reshape(E, D, FC, 128)
    w2 = np.asarray(L0_ffn_w2).reshape(E, FC, 128, D).transpose(0, 2, 1, 3)
    expert_w = np.zeros((E + 1, 128, FC, WB), f32)
    expert_w[:E, :, :, 0:128] = w1[:, :128]
    expert_w[:E, :DR, :, 128:256] = w1[:, 128:]
    expert_w[:E, DR:, :, 128:256] = w1[:, 128:]
    expert_w[1:, :, :, 256:] = w2
    expert_w = expert_w.reshape(E + 1, 128, FC * WB)

    nc = bacc.Bacc("TRN2", target_bir_lowering=False, num_devices=1)
    arrays, args = {}, []
    for name, a in (("xT", xT), ("embed_w", embed_w), ("pos_w", pos_w), ("ident_w", np.eye(128, dtype=f32)), ("att_a", att_a),
                    ("att_b", att_b), ("att_r", att_r), ("expert_w", expert_w)):
        arrays[name] = np.ascontiguousarray(a)
        args.append(nc.dram_tensor(name, a.shape, F32, kind="ExternalInput").ap())
    args.append(nc.dram_tensor("out", (TOK, D), F32, kind="ExternalOutput").ap())
    vit_tower(nc, *args)
    r = run_bass_kernel_spmd(nc, [arrays], core_ids=[0])
    return r.results[0]["out"].reshape(B, N, D)
```
